# Optimizing a Trainium2 kernel written in Bass

```python
import numpy as np
import jax
import jax.numpy as jnp

def _softmax(x, axis=-1):
    return jax.nn.softmax(x, axis=axis)
def _gelu(x):
    return jax.nn.gelu(x, approximate=True)
def _silu(x):
    return jax.nn.silu(x)
def _sigmoid(x):
    return jax.nn.sigmoid(x)
def _layernorm(x, axis=-1, eps=1e-5):
    m = jnp.mean(x, axis=axis, keepdims=True)
    v = jnp.var(x, axis=axis, keepdims=True)
    return (x - m) / jnp.sqrt(v + eps)
def _scatter_add(tgt, idx, src, axis=0):
    return tgt.at[idx].add(src)
def _segment_sum(src, seg, n):
    return jax.ops.segment_sum(src, seg, n)

kernel_name = 'mk_conv_preact_d2_conv_nchw256_d92bb9'

def setup_inputs(seed: int = 0):
    np.random.seed(seed)
    _w = jnp.asarray
    def _rec_inputs():
        import jax
        import jax.numpy as jnp
        _gk = jax.random.key(seed)
        x = -0.0002144 + 1 * jax.random.normal(jax.random.fold_in(_gk, 1), (4, 256, 80, 80), jnp.float32)
        return x
    x = _rec_inputs()
    def _L0_conv_setup():
        import jax, jax.numpy as jnp
        import numpy as np
        from jax import lax
        K = 3

        def _offset_conv(x, w_off):
            return lax.conv_general_dilated(x, w_off, window_strides=(1, 1), padding=((1, 1), (1, 1)), dimension_numbers=('NCHW', 'OIHW', 'NCHW'))

        def _deform_conv(x, offsets, w_deform):
            B, C, H, W = x.shape
            KK = K * K
            off = offsets.reshape(B, KK, 2, H, W)
            dy, dx = (off[:, :, 0], off[:, :, 1])
            kgy = (jnp.arange(K) - 1).repeat(K).astype(x.dtype)
            kgx = jnp.tile(jnp.arange(K) - 1, K).astype(x.dtype)
            base_y = jnp.arange(H, dtype=x.dtype)[:, None]
            base_x = jnp.arange(W, dtype=x.dtype)[None, :]
            py = base_y[None, None] + kgy[None, :, None, None] + dy
            px = base_x[None, None] + kgx[None, :, None, None] + dx
            y0 = jnp.floor(py)
            x0 = jnp.floor(px)
            wy1 = py - y0
            wy0 = 1.0 - wy1
            wx1 = px - x0
            wx0 = 1.0 - wx1

            def gather(yf, xf):
                valid = (yf >= 0) & (yf <= H - 1) & (xf >= 0) & (xf <= W - 1)
                yi = jnp.clip(yf, 0, H - 1).astype(jnp.int32)
                xi = jnp.clip(xf, 0, W - 1).astype(jnp.int32)
                v = jax.vmap(lambda xb, yb, xb2: xb[:, yb, xb2])(x, yi, xi)
                return v * valid[:, None].astype(x.dtype)
            val = (wy0 * wx0)[:, None] * gather(y0, x0) + (wy0 * wx1)[:, None] * gather(y0, x0 + 1) + (wy1 * wx0)[:, None] * gather(y0 + 1, x0) + (wy1 * wx1)[:, None] * gather(y0 + 1, x0 + 1)
            Cout = w_deform.shape[0]
            wk = w_deform.reshape(Cout, C, KK)
            return jnp.einsum('bckhw,ock->bohw', val, wk)
        key = jax.random.key(seed)
        k1, k2, k3 = jax.random.split(key, 3)
        B, C, H, W = (4, 256, 80, 80)
        Cout = 256
        x = jax.random.normal(k1, (B, C, H, W), dtype=jnp.float32)
        w_off = jax.random.normal(k2, (2 * K * K, C, K, K), dtype=jnp.float32) * 0.01
        w_deform = jax.random.normal(k3, (Cout, C, K, K), dtype=jnp.float32) * 0.05
        return {'x': x, 'w_off': w_off, 'w_deform': w_deform}
    _L0_conv_all = _L0_conv_setup()
    _L0_conv_in = {k: v for k, v in _L0_conv_all.items() if k in ('w_off', 'w_deform', )}
    del _L0_conv_all

    def _L1_conv_setup():
        import jax, jax.numpy as jnp
        import numpy as np
        B, C1, C2, H, W = (8, 256, 256, 80, 80)
        E, S = (4, 1)
        key = jax.random.key(seed)
        k1, k2, k3, k4 = jax.random.split(key, 4)
        x = jax.random.normal(k1, (B, C1, H, W), dtype=jnp.float32)
        Wr = jax.random.normal(k2, (C1, E), dtype=jnp.float32) * 0.02
        We = jax.random.normal(k3, (E, C1, C2), dtype=jnp.float32) * 0.02
        Ws = jax.random.normal(k4, (S, C1, C2), dtype=jnp.float32) * 0.02
        return {'x': x, 'Wr': Wr, 'We': We, 'Ws': Ws, 'top_k': 1}
    _L1_conv_all = _L1_conv_setup()
    _L1_conv_in = {k: v for k, v in _L1_conv_all.items() if k in ('Wr', 'We', 'Ws', )}
    del _L1_conv_all

    return {
        "x": x,
        "L0_conv_w_off": _L0_conv_in["w_off"],
        "L0_conv_w_deform": _L0_conv_in["w_deform"],
        "L1_conv_Wr": _L1_conv_in["Wr"],
        "L1_conv_We": _L1_conv_in["We"],
        "L1_conv_Ws": _L1_conv_in["Ws"],
    }

def reference(x, L0_conv_w_off, L0_conv_w_deform, L1_conv_Wr, L1_conv_We, L1_conv_Ws):
    import jax
    import jax.numpy as jnp
    def _L0_conv_ref(x, w_off, w_deform):
        import jax, jax.numpy as jnp
        import numpy as np
        from jax import lax
        K = 3

        def _offset_conv(x, w_off):
            return lax.conv_general_dilated(x, w_off, window_strides=(1, 1), padding=((1, 1), (1, 1)), dimension_numbers=('NCHW', 'OIHW', 'NCHW'))

        def _deform_conv(x, offsets, w_deform):
            B, C, H, W = x.shape
            KK = K * K
            off = offsets.reshape(B, KK, 2, H, W)
            dy, dx = (off[:, :, 0], off[:, :, 1])
            kgy = (jnp.arange(K) - 1).repeat(K).astype(x.dtype)
            kgx = jnp.tile(jnp.arange(K) - 1, K).astype(x.dtype)
            base_y = jnp.arange(H, dtype=x.dtype)[:, None]
            base_x = jnp.arange(W, dtype=x.dtype)[None, :]
            py = base_y[None, None] + kgy[None, :, None, None] + dy
            px = base_x[None, None] + kgx[None, :, None, None] + dx
            y0 = jnp.floor(py)
            x0 = jnp.floor(px)
            wy1 = py - y0
            wy0 = 1.0 - wy1
            wx1 = px - x0
            wx0 = 1.0 - wx1

            def gather(yf, xf):
                valid = (yf >= 0) & (yf <= H - 1) & (xf >= 0) & (xf <= W - 1)
                yi = jnp.clip(yf, 0, H - 1).astype(jnp.int32)
                xi = jnp.clip(xf, 0, W - 1).astype(jnp.int32)
                v = jax.vmap(lambda xb, yb, xb2: xb[:, yb, xb2])(x, yi, xi)
                return v * valid[:, None].astype(x.dtype)
            val = (wy0 * wx0)[:, None] * gather(y0, x0) + (wy0 * wx1)[:, None] * gather(y0, x0 + 1) + (wy1 * wx0)[:, None] * gather(y0 + 1, x0) + (wy1 * wx1)[:, None] * gather(y0 + 1, x0 + 1)
            Cout = w_deform.shape[0]
            wk = w_deform.reshape(Cout, C, KK)
            return jnp.einsum('bckhw,ock->bohw', val, wk)
        offsets = _offset_conv(x, w_off)
        return _deform_conv(x, offsets, w_deform)

    def _L1_conv_ref(x, Wr, We, Ws, top_k):
        import jax, jax.numpy as jnp
        import numpy as np
        B, C1, C2, H, W = (8, 256, 256, 80, 80)
        E, S = (4, 1)
        b, c, h, w = x.shape
        n = b * h * w
        t = x.transpose(0, 2, 3, 1).reshape(n, c)
        probs = jax.nn.softmax(t @ Wr, axis=-1)
        vals, idx = jax.lax.top_k(probs, top_k)
        wts = vals / jnp.sum(vals, axis=-1, keepdims=True)
        gate = jnp.zeros_like(probs).at[jnp.arange(n)[:, None], idx].set(wts)
        y = jnp.einsum('nc,ecd->end', t, We)
        routed = jnp.einsum('ne,end->nd', gate, y)
        shared = jnp.einsum('nc,scd->nd', t, Ws) / Ws.shape[0]
        out = (routed + shared).reshape(b, h, w, -1).transpose(0, 3, 1, 2)
        return out

    def _gn(v, G=32, eps=1e-5):
        B_, C_, H_, W_ = v.shape
        g = v.reshape(B_, G, C_ // G, H_, W_)
        m = jnp.mean(g, axis=(2, 3, 4), keepdims=True)
        s = jnp.var(g, axis=(2, 3, 4), keepdims=True)
        return ((g - m) / jnp.sqrt(s + eps)).reshape(v.shape)

    def _ln_c(v, eps=1e-6):
        m = jnp.mean(v, axis=1, keepdims=True)
        s = jnp.var(v, axis=1, keepdims=True)
        return (v - m) / jnp.sqrt(s + eps)

    def _ln_t(v, eps=1e-5):
        m = jnp.mean(v, axis=-1, keepdims=True)
        s = jnp.var(v, axis=-1, keepdims=True)
        return (v - m) / jnp.sqrt(s + eps)

    def _to_tokens(v):
        B_, C_, H_, W_ = v.shape
        return v.reshape(B_, C_, H_ * W_).transpose(0, 2, 1)
    def _from_tokens(t, like):
        B_, C_, H_, W_ = like.shape
        return t.transpose(0, 2, 1).reshape(B_, C_, H_, W_)

    x = x + _L0_conv_ref(_gn(x), L0_conv_w_off, L0_conv_w_deform)
    x = x + _L1_conv_ref(_gn(x), L1_conv_Wr, L1_conv_We, L1_conv_Ws, 1)
    return x


_drawn_inputs = setup_inputs


def setup_inputs(seed=0):
    import zlib

    import numpy as np

    out = dict(_drawn_inputs(seed))
    spreads = {}
    factors = {}
    for name, (base, spread) in spreads.items():
        noise = np.random.default_rng([zlib.crc32(name.encode()), seed]).standard_normal(out[name].shape)
        drawn = base * np.exp(spread * noise) if base else spread * noise
        out[name] = jnp.asarray(drawn.astype(out[name].dtype))
    for name, factor in factors.items():
        out[name] = (out[name] * factor).astype(out[name].dtype)
    return out
```

```python
from contextlib import ExitStack

import concourse.bass as bass
from concourse import mybir

F32 = mybir.dt.float32
BF16 = mybir.dt.bfloat16
I32 = mybir.dt.int32
U32 = mybir.dt.uint32
ALU = mybir.AluOpType
ACT = mybir.ActivationFunctionType
AX = mybir.AxisListType

P = 128
IMAGES, CH, SIDE = 4, 256, 80
HALVES = CH // P
TAPS = 9
PATCH = 16
STRIPS = SIDE // PATCH
COLS = SIDE // PATCH
TILES = 2
PIX = PATCH * PATCH
STRIP_PIX = PATCH * SIDE
STRIP_TILES = COLS * TILES
EXPERTS = 4
OFFS = 2 * TAPS
GROUP = 8

RIM = 2
WIDE = SIDE + 2 * RIM
ENTRIES = (SIDE + 2 * RIM - 1) * WIDE
TROW = 112
TURNS = WIDE * PATCH // TROW
CHUNK = 3

PAIRS = COLS * TAPS
UNITS = PAIRS * TILES
RING = 9
STRIP_RING = STRIPS + 1
QUADS = 4
PART_ROUNDS = -(-TAPS * HALVES // QUADS)
PART_SLOTS = PART_ROUNDS + 2
STAT_PIX = 320
STAT_PIECES = SIDE * SIDE // STAT_PIX
PREP = 15
STAGE = 3 * HALVES
EPS = 1e-5
START = 1


class Step:

    def __init__(self, b):
        self.sample = b if 0 <= b < IMAGES else None
        self.table = b + 1 if 0 <= b + 1 < IMAGES else None
        self.refill = b + 2 if b + 2 < IMAGES else None
        self.expert = b - 1 if 0 <= b - 1 < IMAGES else None
        self.only_refill = b == -2


STEPS = [Step(b) for b in range(-2, IMAGES + 1)]


def each_strip(eng, step, body):
    if not step.only_refill:
        with eng.Fori(0, STRIPS - 1) as s:
            body(s, False)
    body(STRIPS - 1, True)


def gn_chains():
    at, n = {}, 0
    for i, step in enumerate(STEPS):
        if step.refill is not None:
            at[i, "x"] = n
            n += 1
        if step.sample is not None:
            at[i, "x1"] = n
            n += 1
    return at


GN_A, GN_B, GN_C = 4, 4, 3
GN_OPS = GN_A + GN_B + GN_C


def build(nc, x, w_offset, w_deform, w_router, w_expert, w_shared, ident, group_mean, position,
          strip_row, first_wins, sum_parts, out):
    chain_of = gn_chains()
    tables = [nc.dram_tensor(f"table{b}", [ENTRIES, 2 * CH], F32, kind="Internal") for b in range(IMAGES)]

    with ExitStack() as ctx:
        def sb(name, shape, dt=F32):
            return ctx.enter_context(nc.sbuf_tensor(name, shape, dt))

        def pb(name, shape):
            return ctx.enter_context(nc.psum_tensor(name, shape, F32))

        def sem(name):
            return ctx.enter_context(nc.semaphore(name))

        idn = sb("idn", [P, P])
        idn_bf = sb("idn_bf", [P, P], BF16)
        gmean = sb("gmean", [P, P])
        posc = sb("posc", [P, 2, STRIP_TILES * TAPS])
        srow = sb("srow", [P, STRIPS])
        order = sb("order", [P, TILES, EXPERTS])
        woff = sb("woff", [P, TAPS * HALVES, P // QUADS])
        pick = sb("pick", [P, OFFS])
        wdef = sb("wdef", [P, TAPS * HALVES, CH])
        wrt = sb("wrt", [P, HALVES, EXPERTS])
        wexp = sb("wexp", [P, EXPERTS * HALVES, CH])
        xin = sb("xin", [P, HALVES, SIDE + 2, SIDE])
        strip = sb("strip", [P, HALVES, PATCH + 2, WIDE])
        turned = sb("turned", [TROW, CHUNK, CH])
        stat_x = sb("stat_x", [P, HALVES, STAT_PIECES, 6])
        part = sb("part", [P, PIX])
        pyx = sb("pyx", [P, 2, STRIP_TILES * TAPS])
        whole = sb("whole", [P, 2, STRIP_TILES * TAPS], I32)
        floor = sb("floor", [P, 2, STRIP_TILES * TAPS])
        tmp = whole[:, :, :].bitcast(F32)
        w_far = sb("w_far", [P, 2, STRIP_TILES * TAPS])
        w_near = pyx
        entry_img = sb("entry_img", [P, STRIPS * STRIP_TILES, TAPS], U32)
        weight_img = sb("weight_img", [P, STRIPS * STRIP_TILES, TAPS, 4])
        entry = [sb(f"entry{j}", [P, TILES, TAPS], U32) for j in range(COLS)]
        weight = [sb(f"weight{j}", [P, TILES, TAPS, 4]) for j in range(COLS)]
        corners = sb("corners", [P, RING, 4 * CH])
        val = sb("val", [P, 2, HALVES, PIX])
        x1 = sb("x1", [P, STRIP_RING, HALVES, PATCH, SIDE])
        stat_x1 = sb("stat_x1", [P, HALVES, STRIPS * COLS, 6])
        xn = sb("xn", [P, HALVES, PIX])
        xm = sb("xm", [P, 2, HALVES, PIX])
        top = sb("top", [P, TILES])
        score = sb("score", [P, TILES, EXPERTS])
        mask = sb("mask", [P, TILES, EXPERTS], BF16)
        mv = sb("mv", [P, HALVES, 2])
        sq = sb("sq", [P, HALVES])
        gmv = sb("gmv", [P, HALVES, 2])
        gsq = sb("gsq", [P, HALVES])
        gvar = sb("gvar", [P, HALVES])
        root = sb("root", [P, HALVES])
        scale_x = sb("scale_x", [P, HALVES])
        shift_x = sb("shift_x", [P, HALVES])
        shift_below = sb("shift_below", [P, STRIPS, HALVES])
        zero = sb("zero", [P, 1])
        scale_x1 = sb("scale_x1", [P, HALVES])
        shift_x1 = sb("shift_x1", [P, HALVES])

        p_turn = [pb(f"p_turn{i}", [P, HALVES * PIX]) for i in range(2)]
        p_acc = [pb(f"p_acc{i}", [P, HALVES * PIX]) for i in range(2)]
        p_part = pb("p_part", [P, PIX + STRIP_TILES * OFFS])
        p_offs = p_part[:, PIX:PIX + STRIP_TILES * OFFS]
        p_table = pb("p_table", [P, CH])
        p_mask = pb("p_mask", [P, 2, PIX])
        p_moe = pb("p_moe", [P, HALVES * PIX])

        consts_in = sem("consts_in")
        weights_in = sem("weights_in")
        zeroed = sem("zeroed")
        consts_made = sem("consts_made")
        rim_out = sem("rim_out")
        x_in = [sem(f"x_in{i}") for i in range(STRIPS)]
        x_stats = sem("x_stats")
        gn_dve = sem("gn_dve")
        gn_sums = sem("gn_sums")
        gn_root = sem("gn_root")
        staged = sem("staged")
        part_done = sem("part_done")
        part_copied = sem("part_copied")
        offs_done = sem("offs_done")
        table_turned = sem("table_turned")
        table_copied = sem("table_copied")
        table_out = sem("table_out")
        prepped = sem("prepped")
        picked = sem("picked")
        gathered = [sem(f"gathered{i}") for i in range(RING)]
        unit_free = sem("unit_free")
        unit_taken = sem("unit_taken")
        scaled = sem("scaled")
        blended = sem("blended")
        val_ready = sem("val_ready")
        conv_done = sem("conv_done")
        resid_in = sem("resid_in")
        x1_done = sem("x1_done")
        x1_stats = sem("x1_stats")
        xn_ready = sem("xn_ready")
        logits_done = sem("logits_done")
        routed = sem("routed")
        mask_done = sem("mask_done")
        xm_ready = sem("xm_ready")
        moe_done = sem("moe_done")
        out_ready = sem("out_ready")
        out_stored = sem("out_stored")

        ROUTE = 5
        ZEROED = 6
        CONSTS = 8

        started = {
            "sync": [(table_out, 16), (out_stored, 16)],
            "scalar": [(val_ready, 1), (part_copied, 1), (table_copied, 1)],
            "tensor": [(conv_done, 1), (mask_done, 1), (moe_done, 1)],
            "vector": [(x1_done, 1), (xm_ready, 1), (out_ready, 1), (prepped, 1)],
        }

        def start(eng, name):
            for counter, unit in started[name]:
                eng.sem_inc(counter, START * unit)

        def reuse(n, l):
            return n if isinstance(l, int) and l == 0 else n - 1

        block = ctx.enter_context(nc.Block())

        @block.sync
        def _(sp):
            start(sp, "sync")
            sp.dma_start(idn[:, :], ident).then_inc(consts_in, 16)
            sp.dma_start(gmean[:, :], group_mean).then_inc(consts_in, 16)
            sp.dma_start(posc[:, :, :], position).then_inc(consts_in, 16)
            sp.dma_start(srow[:, :], strip_row).then_inc(consts_in, 16)
            sp.dma_start(order[:, :, :], first_wins).then_inc(consts_in, 16)
            sp.dma_start(wrt[:, :, :], w_router).then_inc(consts_in, 16)
            sp.dma_start(pick[:, :], sum_parts).then_inc(consts_in, 16)
            sp.wait_ge(zeroed, ZEROED)
            sp.dma_start(woff[:, :, 0:OFFS], w_offset).then_inc(consts_in, 16)

            def load_x(image, i):
                sp.dma_start(xin[:, :, 1 + PATCH * i:1 + PATCH * (i + 1), :].rearrange("p h r c -> p h (r c)"),
                             x[image, :, :, STRIP_PIX * i:STRIP_PIX * (i + 1)].rearrange("h p n -> p h n")
                             ).then_inc(x_in[i], 16)

            def rims():
                zeros = strip[0:WIDE, 0, :, :].rearrange("p r c -> p (r c)")
                for t in tables:
                    last = ENTRIES - WIDE
                    sp.dma_start(t[0:WIDE, :], zeros[:, 0:2 * CH]).then_inc(rim_out, 16)
                    sp.dma_start(t[WIDE:2 * WIDE, 0:CH], zeros[:, 0:CH]).then_inc(rim_out, 16)
                    sp.dma_start(t[last - WIDE:last, CH:2 * CH], zeros[:, 0:CH]).then_inc(rim_out, 16)
                    sp.dma_start(t[last:ENTRIES, :], zeros[:, 0:2 * CH]).then_inc(rim_out, 16)

            def strip_body(step, s, last):
                if step.sample is not None:
                    q = STRIPS * step.sample + s
                    if step.expert is not None:
                        sp.wait_ge(out_stored, 16 * START + (q - STRIPS) * 16)
                    sp.dma_start(x1[:, bass.ds(q % STRIP_RING, 1), :, :, :].rearrange("p o h r c -> p (o h) (r c)"),
                                 x[step.sample, :, :, bass.ds(STRIP_PIX * s, STRIP_PIX)].rearrange("h p n -> p h n")
                                 ).then_inc(resid_in, 16)
                if last and step.refill is not None:
                    if step.table is not None:
                        sp.wait_ge(staged, STAGE * STRIPS * (step.table + 1))
                    for i in range(STRIPS):
                        if step.sample is not None:
                            sp.wait_ge(conv_done, START + PAIRS * (STRIPS * step.sample + s) + 2 * i + 1)
                        load_x(step.refill, i)
                if step.table is not None:
                    t = tables[step.table]
                    for c in range(TURNS // CHUNK):
                        sp.wait_ge(table_copied, START + TURNS * (STRIPS * step.table + s) + CHUNK * (c + 1))
                        f = (PATCH * s + RIM) * WIDE + TROW * CHUNK * c
                        src = turned[:, :, :]
                        sp.dma_start(t[bass.ds(f, TROW * CHUNK), 0:CH].rearrange("(i p) c -> p i c", p=TROW),
                                     src).then_inc(table_out, 16)
                        sp.dma_start(t[bass.ds(f - WIDE, TROW * CHUNK), CH:2 * CH].rearrange("(i p) c -> p i c", p=TROW),
                                     src).then_inc(table_out, 16)
                if step.expert is not None:
                    q = STRIPS * step.expert + s
                    sp.wait_ge(out_ready, START + COLS * (q + 1))
                    sp.dma_start(out[step.expert, :, :, bass.ds(STRIP_PIX * s, STRIP_PIX)].rearrange("h p n -> p h n"),
                                 x1[:, bass.ds(q % STRIP_RING, 1), :, :, :].rearrange("p o h r c -> p (o h) (r c)")
                                 ).then_inc(out_stored, 16)

            for i, step in enumerate(STEPS):
                each_strip(sp, step, lambda s, last: strip_body(step, s, last))
                if step.only_refill:
                    rims()
                    sp.dma_start(wdef[:, :, :], w_deform).then_inc(weights_in, 16)
                    sp.dma_start(wexp[:, :, :], w_expert).then_inc(weights_in, 16)
                    sp.dma_start(xm[:, 0, :, :], w_shared).then_inc(weights_in, 16)
            sp.wait_ge(out_stored, 16 * START + 16 * STRIPS * IMAGES)

        @block.gpsimd
        def _(pool):
            nc.gpsimd.memset(strip[:, :, :, :], 0.0).then_inc(zeroed, 1)
            nc.gpsimd.memset(xin[:, :, 0:1, :], 0.0).then_inc(zeroed, 1)
            nc.gpsimd.memset(xin[:, :, SIDE + 1:SIDE + 2, :], 0.0).then_inc(zeroed, 1)
            nc.gpsimd.memset(shift_below[:, :, :], 0.0).then_inc(zeroed, 1)
            nc.gpsimd.memset(zero[:, :], 0.0).then_inc(zeroed, 1)
            nc.gpsimd.memset(woff[:, :, :], 0.0).then_inc(zeroed, 1)
            nc.gpsimd.memset(corners[:, 0, 0:1], 0.0).then_inc(unit_free, RING)
            pool.wait_ge(unit_free, RING)

            def strip_body(step, s, last):
                q = STRIPS * step.sample + s
                for j in range(COLS):
                    g = COLS * q + j
                    tile = STRIP_TILES * s + TILES * j
                    nc.gpsimd.tensor_copy(entry[j][:, :, :], entry_img[:, bass.ds(tile, TILES), :]).then_inc(picked, 1)
                    nc.gpsimd.tensor_copy(weight[j][:, :, :, :].rearrange("p t k c -> p t (k c)"),
                                          weight_img[:, bass.ds(tile, TILES), :, :].rearrange("p t k c -> p t (k c)")
                                          ).then_inc(picked, 1)
                    pool.wait_ge(picked, 2 * (g + 1))
                    for v in range(UNITS // COLS):
                        k, t = divmod(v, TILES)
                        local = UNITS // COLS * j + v
                        pool.wait_ge(unit_free, UNITS * q + local + 1).then_inc(unit_taken, 1)
                        nc.gpsimd.indirect_dma_start(
                            corners[:, local % RING, :], None, tables[step.sample][:, :],
                            bass.IndirectOffsetOnAxis(ap=entry[j][:, t, k:k + 1], axis=0),
                        ).then_inc(gathered[local % RING], 16)

            for step in STEPS:
                if step.sample is not None:
                    pool.wait_ge(prepped, START + PREP * STRIPS * (step.sample + 1))
                    pool.wait_ge(rim_out, 16 * 4 * IMAGES)
                    pool.wait_ge(table_out, 16 * START + 16 * 2 * (TURNS // CHUNK) * STRIPS * (step.sample + 1))
                    each_strip(pool, step, lambda s, last: strip_body(step, s, last))

        @block.scalar
        def _(act):
            start(act, "scalar")
            act.wait_ge(zeroed, ZEROED)

            def scale_corner(q, l):
                j, k = divmod(l % PAIRS, TAPS)
                for t in range(TILES):
                    local = TILES * (l % PAIRS) + t
                    act.wait_ge(gathered[local % RING], 16 * (UNITS // RING * (q + l // PAIRS) + local // RING + 1))
                    c = corners[:, local % RING, 0:CH]
                    nc.scalar.activation(c, c, ACT.Identity, bias=zero[:, 0:1],
                                         scale=weight[j][:, t, k, 0:1]).then_inc(scaled, 1)

            def copy_val(q, l):
                n = PAIRS * q + l
                act.wait_ge(unit_free, RING + TILES * (n + 1))
                act.wait_ge(conv_done, START + reuse(n, l % PAIRS))
                b = l % PAIRS % 2
                nc.scalar.activation(val[:, b, :, :].rearrange("p h n -> p (h n)"), p_turn[b][:, :],
                                     ACT.Copy).then_inc(val_ready, 1)

            def stage(s, piece, edge_row):
                h, piece = divmod(piece, 3)
                sc = scale_x[:, h:h + 1]
                cols = slice(RIM, RIM + SIDE)
                if piece == 0:
                    nc.scalar.activation(strip[:, h, 1:1 + PATCH, cols], xin[:, h, bass.ds(PATCH * s + 1, PATCH), :],
                                         ACT.Identity, bias=shift_x[:, h:h + 1], scale=sc).then_inc(staged, 1)
                elif piece == 1:
                    bias = zero[:, 0:1] if edge_row else shift_x[:, h:h + 1]
                    nc.scalar.activation(strip[:, h, 0:1, cols], xin[:, h, bass.ds(PATCH * s, 1), :],
                                         ACT.Identity, bias=bias, scale=sc).then_inc(staged, 1)
                else:
                    nc.scalar.activation(strip[:, h, 1 + PATCH:2 + PATCH, cols],
                                         xin[:, h, bass.ds(PATCH * (s + 1) + 1, 1), :], ACT.Identity,
                                         bias=shift_below[:, bass.ds(s, 1), h], scale=sc).then_inc(staged, 1)

            def gn_take_root(chain):
                act.wait_ge(gn_dve, GN_OPS * chain + GN_A + GN_B)
                nc.scalar.activation(root[:, :], gvar[:, :], ACT.Sqrt).then_inc(gn_root, 1)

            def strip_body(i, step, s, last):
                for j in range(COLS):
                    for k in range(TAPS):
                        l = TAPS * j + k
                        if step.sample is not None:
                            q = STRIPS * step.sample + s
                            if not (last and l + 3 >= PAIRS):
                                scale_corner(q, l + 3)
                            if not (last and l + 1 >= PAIRS):
                                copy_val(q, l + 1)
                        if step.table is not None and j < TURNS // CHUNK and k % 3 == 1:
                            q = STRIPS * step.table + s
                            turn = CHUNK * j + k // 3
                            act.wait_ge(table_turned, TURNS * q + turn + 1)
                            if k == 1:
                                act.wait_ge(table_out, 16 * START + 16 * 2 * (TURNS // CHUNK * q + j))
                            nc.scalar.activation(turned[:, turn % CHUNK, :], p_table[0:TROW, :],
                                                 ACT.Copy).then_inc(table_copied, 1)
                        if step.table is not None and l < PART_SLOTS * COLS and l % PART_SLOTS == PART_ROUNDS:
                            g = COLS * (STRIPS * step.table + s) + l // PART_SLOTS
                            act.wait_ge(part_done, g + 1)
                            nc.scalar.activation(part[:, :], p_part[:, 0:PIX], ACT.Copy).then_inc(part_copied, 1)
                        if step.expert is not None and k == 0:
                            q = STRIPS * step.expert + s
                            g = COLS * q + j
                            if j == 0:
                                act.wait_ge(gn_dve, GN_OPS * (chain_of[i - 1, "x1"] + 1))
                            act.wait_ge(xm_ready, START + EXPERTS * g)
                            for h in range(HALVES):
                                nc.scalar.activation(
                                    xn[:, h, :].rearrange("p (r c) -> p r c", c=PATCH),
                                    x1[:, bass.ds(q % STRIP_RING, 1), h, :, PATCH * j:PATCH * (j + 1)]
                                    .rearrange("p o r c -> p (o r) c"),
                                    ACT.Identity, bias=shift_x1[:, h:h + 1], scale=scale_x1[:, h:h + 1]
                                ).then_inc(xn_ready, 1)
                        if j == COLS - 1:
                            if last and step.refill is not None:
                                if k == 5:
                                    gn_take_root(chain_of[i, "x"])
                                if k == 8:
                                    act.wait_ge(gn_dve, GN_OPS * (chain_of[i, "x"] + 1))
                                    if step.table is not None:
                                        act.wait_ge(offs_done, STRIPS * (step.table + 1))
                                    else:
                                        act.wait_ge(rim_out, 16 * 4 * IMAGES)
                                    for piece in range(STAGE):
                                        stage(0, piece, True)
                            elif not last and step.table is not None and 2 <= k < 2 + STAGE:
                                act.wait_ge(offs_done, STRIPS * step.table + s + 1)
                                stage(s + 1, k - 2, False)

            for i, step in enumerate(STEPS):
                if step.sample is not None:
                    for l in range(3):
                        scale_corner(STRIPS * step.sample, l)
                    copy_val(STRIPS * step.sample, 0)
                each_strip(act, step, lambda s, last: strip_body(i, step, s, last))
                if step.sample is not None:
                    gn_take_root(chain_of[i, "x1"])

        @block.tensor
        def _(pe):
            start(pe, "tensor")
            pe.wait_ge(consts_in, 16 * CONSTS)

            def turn_pair(q, l):
                n = PAIRS * q + l
                l = l % PAIRS
                pe.wait_ge(val_ready, START + reuse(n, l))
                for t in range(TILES):
                    pe.wait_ge(blended, 6 * n + 5 + t)
                    unit = (TILES * l + t) % RING
                    for h in range(HALVES):
                        mm = nc.tensor.transpose(p_turn[l % 2][:, PIX * h + P * t:PIX * h + P * (t + 1)],
                                                 corners[:, unit, P * h:P * (h + 1)], idn[:, :])
                    mm.then_inc(unit_free, 1)

            def conv_pair(q, l):
                j, k = divmod(l, TAPS)
                n = PAIRS * q + l
                pe.wait_ge(val_ready, START + n + 1)
                if k == 0:
                    pe.wait_ge(x1_done, START + COLS * q + (j if j == 0 else j - 1))
                for m in range(HALVES):
                    for h in range(HALVES):
                        mm = nc.tensor.matmul(p_acc[j % 2][:, PIX * m:PIX * (m + 1)],
                                              wdef[:, HALVES * k + h, P * m:P * (m + 1)], val[:, l % 2, h, :],
                                              start=(k == 0 and h == 0 and m == 0), stop=(k == TAPS - 1),
                                              skip_group_check=True)
                mm.then_inc(conv_done, 1)

            def offset_part(q, l):
                j, i = divmod(l, PART_SLOTS)
                g = COLS * q + j
                if i < PART_ROUNDS:
                    if i == 0:
                        pe.wait_ge(part_copied, START + g)
                    for kh in range(QUADS * i, min(QUADS * (i + 1), TAPS * HALVES)):
                        k, h = divmod(kh, HALVES)
                        c = P // QUADS * (kh % QUADS)
                        row, col = k // 3, PATCH * j + k % 3 + RIM - 1
                        mm = nc.tensor.matmul(p_part[c:c + P // QUADS, 0:PIX], woff[:, kh, :],
                                              strip[:, h, row:row + PATCH, col:col + PATCH],
                                              start=(i == 0), stop=(kh + QUADS >= TAPS * HALVES))
                    if i == PART_ROUNDS - 1:
                        mm.then_inc(part_done, 1)
                elif i == PART_ROUNDS + 1:
                    pe.wait_ge(part_copied, START + g + 1)
                    for t in range(TILES):
                        at = OFFS * (TILES * j + t)
                        mm = nc.tensor.matmul(p_offs[:, at:at + OFFS], part[:, P * t:P * (t + 1)], pick[:, :],
                                              start=True, stop=True)
                    if j == COLS - 1:
                        mm.then_inc(offs_done, 1)

            def table_turn(q, turn):
                pe.wait_ge(table_copied, START + TURNS * q + turn)
                for h in range(HALVES):
                    rows = strip[:, h, :, :].rearrange("p r c -> p (r c)")
                    at = WIDE + TROW * turn
                    mm = nc.tensor.transpose(p_table[0:TROW, P * h:P * (h + 1)],
                                             rows[:, at:at + TROW], idn[:, :])
                mm.then_inc(table_turned, 1)

            def gn_group_sums(chain, tables_done):
                pe.wait_ge(gn_dve, GN_OPS * chain + GN_A)
                pe.wait_ge(table_copied, START + tables_done)
                nc.tensor.matmul(p_table[:, 0:2 * HALVES], gmean[:, :],
                                 mv[:, :, :].rearrange("p h v -> p (h v)"), start=True, stop=True
                                 ).then_inc(gn_sums, 1)

            def expert_part(q, j, k):
                g = COLS * q + j
                if k == 1:
                    pe.wait_ge(xn_ready, HALVES * (g + 1))
                    pe.wait_ge(out_ready, START + g)
                    for t in range(TILES):
                        for h in range(HALVES):
                            mm = nc.tensor.matmul(p_moe[:, EXPERTS * t:EXPERTS * (t + 1)], xn[:, h, P * t:P * (t + 1)],
                                                  wrt[:, h, :], start=(h == 0), stop=(h == HALVES - 1))
                    mm.then_inc(logits_done, 1)
                if k == 3 or k == 5:
                    if k == 5:
                        expert_products(g, 0)
                        expert_products(g, 1)
                    first = k - 3
                    pe.wait_ge(routed, ROUTE * (g + 1))
                    pe.wait_ge(xm_ready, START + EXPERTS * g + first)
                    for e in range(2):
                        for t in range(TILES):
                            mm = nc.tensor.matmul(p_mask[:, e, P * t:P * (t + 1)],
                                                  mask[:, t, first + e:first + e + 1].to_broadcast([P, P]),
                                                  idn_bf[:, :], start=True, stop=True)
                    mm.then_inc(mask_done, 1)
                if k == 7:
                    expert_products(g, 2)
                    expert_products(g, 3)

            def expert_products(g, e):
                pe.wait_ge(xm_ready, START + EXPERTS * g + e + 1)
                for m in range(HALVES):
                    for h in range(HALVES):
                        mm = nc.tensor.matmul(p_moe[:, PIX * m:PIX * (m + 1)],
                                              wexp[:, HALVES * e + h, P * m:P * (m + 1)], xm[:, e % 2, h, :],
                                              start=(e == 0 and h == 0 and m == 0), stop=(e == EXPERTS - 1),
                                              skip_group_check=True)
                mm.then_inc(moe_done, 1)

            def strip_body(i, step, s, last):
                if step.table is not None:
                    q = STRIPS * step.table + s
                    pe.wait_ge(staged, STAGE * (q + 1))
                    pe.wait_ge(prepped, START + PREP * q)
                for j in range(COLS):
                    for k in range(TAPS):
                        l = TAPS * j + k
                        if step.sample is not None:
                            q = STRIPS * step.sample + s
                            if not (last and l + 1 >= PAIRS):
                                turn_pair(q, l + 1)
                            conv_pair(q, l)
                        if step.table is not None and j < COLS - 1:
                            q = STRIPS * step.table + s
                            if k % 3 == 0:
                                table_turn(q, CHUNK * j + k // 3)
                            if l < PART_SLOTS * COLS:
                                offset_part(q, l)
                        if step.expert is not None:
                            expert_part(STRIPS * step.expert + s, j, k)
                        if last and step.refill is not None and l == TAPS * (COLS - 1) + 4:
                            done = 0 if step.table is None else TURNS * STRIPS * (step.table + 1)
                            gn_group_sums(chain_of[i, "x"], done)

            for i, step in enumerate(STEPS):
                if step.sample is not None:
                    if step.sample == 0:
                        pe.wait_ge(weights_in, 16 * 3)
                        pe.wait_ge(consts_made, 2)
                    turn_pair(STRIPS * step.sample, 0)
                each_strip(pe, step, lambda s, last: strip_body(i, step, s, last))
                if step.sample is not None:
                    tables_done = TURNS * STRIPS * min(step.sample + 2, IMAGES)
                    gn_group_sums(chain_of[i, "x1"], tables_done)

        @block.vector
        def _(dve):
            start(dve, "vector")
            dve.wait_ge(consts_in, 16 * CONSTS)
            nc.vector.tensor_copy(idn_bf[:, :], idn[:, :]).then_inc(consts_made, 1)

            def blend(q, l):
                n = PAIRS * q + l
                l = l % PAIRS
                j, k = divmod(l, TAPS)
                for c in range(1, 4):
                    for t in range(TILES):
                        unit = (TILES * l + t) % RING
                        if c == 1:
                            dve.wait_ge(scaled, TILES * n + t + 1)
                        else:
                            dve.wait_ge(blended, 6 * n + 2 * (c - 2) + t + 1)
                        acc = corners[:, unit, 0:CH]
                        nc.vector.scalar_tensor_tensor(
                            out=acc, in0=corners[:, unit, CH * c:CH * (c + 1)], scalar=weight[j][:, t, k, c:c + 1],
                            in1=acc, op0=ALU.mult, op1=ALU.add).then_inc(blended, 1)

            def finish_patch(q, s, j):
                g = COLS * q + j
                dve.wait_ge(conv_done, START + TAPS * (g + 1))
                if j == 0:
                    dve.wait_ge(resid_in, 16 * (q + 1))
                at = x1[:, bass.ds(q % STRIP_RING, 1), :, :, PATCH * j:PATCH * (j + 1)].rearrange(
                    "p o h r c -> p (o h) r c")
                nc.vector.tensor_tensor(at, p_acc[j % 2][:, :].rearrange("p (h r c) -> p h r c", h=HALVES, c=PATCH),
                                        at, ALU.add).then_inc(x1_done, 1)
                dve.wait_ge(x1_done, START + g + 1)
                for h in range(HALVES):
                    nc.vector.bn_stats(stat_x1[:, h, bass.ds(COLS * s + j, 1), :],
                                       x1[:, bass.ds(q % STRIP_RING, 1), h, :, PATCH * j:PATCH * (j + 1)]
                                       .rearrange("p o r c -> p (o r) c")).then_inc(x1_stats, 1)

            def prepare(q, s, op):
                offs = p_offs.rearrange("p (n v) -> p v n", v=2)
                row = bass.ds(STRIP_TILES * s, STRIP_TILES)
                if op == 0:
                    dve.wait_ge(offs_done, q + 1)
                elif op != 1:
                    dve.wait_ge(prepped, START + PREP * q + op)
                if op == 0:
                    ins = nc.vector.scalar_tensor_tensor(out=pyx[:, 0, :], in0=posc[:, 0, :], scalar=srow[:, bass.ds(s, 1)],
                                                         in1=offs[:, 0, :], op0=ALU.add, op1=ALU.add)
                elif op == 1:
                    ins = nc.vector.tensor_tensor(pyx[:, 1, :], posc[:, 1, :], offs[:, 1, :], ALU.add)
                elif op == 2:
                    ins = nc.vector.tensor_scalar(pyx[:, :, :], pyx[:, :, :], float(-RIM), SIDE + 0.5, ALU.max, ALU.min)
                elif op == 3:
                    ins = nc.vector.tensor_copy(whole[:, :, :], pyx[:, :, :])
                elif op == 4:
                    ins = nc.vector.tensor_copy(floor[:, :, :], whole[:, :, :])
                elif op == 5:
                    ins = nc.vector.tensor_tensor(tmp[:, :, :], floor[:, :, :], pyx[:, :, :], ALU.is_gt)
                elif op == 6:
                    ins = nc.vector.tensor_tensor(floor[:, :, :], floor[:, :, :], tmp[:, :, :], ALU.subtract)
                elif op == 7:
                    ins = nc.vector.tensor_tensor(w_far[:, :, :], pyx[:, :, :], floor[:, :, :], ALU.subtract)
                elif op == 8:
                    ins = nc.vector.tensor_scalar(w_near[:, :, :], w_far[:, :, :], -1.0, 1.0, ALU.mult, ALU.add)
                elif op == 9:
                    ins = nc.vector.scalar_tensor_tensor(out=tmp[:, 0, :], in0=floor[:, 0, :], scalar=float(WIDE),
                                                         in1=floor[:, 1, :], op0=ALU.mult, op1=ALU.add)
                elif op == 10:
                    ins = nc.vector.tensor_scalar(entry_img[:, row, :].rearrange("p t k -> p (t k)"), tmp[:, 0, :],
                                                  float(RIM * WIDE + RIM), None, ALU.add)
                else:
                    c = op - 11
                    wy = w_far if c % 2 else w_near
                    wx = w_far if c // 2 else w_near
                    ins = nc.vector.tensor_tensor(weight_img[:, row, :, c].rearrange("p t k -> p (t k)"),
                                                  wy[:, 0, :], wx[:, 1, :], ALU.mult)
                ins.then_inc(prepped, 1)

            def route(g):
                logits = p_moe[:, 0:TILES * EXPERTS].rearrange("p (t e) -> p t e", e=EXPERTS)
                best = top[:, :].rearrange("p (t o) -> p t o", o=1).to_broadcast([P, TILES, EXPERTS])
                dve.wait_ge(logits_done, g + 1)
                nc.vector.tensor_reduce(top[:, :], logits, AX.X, ALU.max).then_inc(routed, 1)
                dve.wait_ge(routed, ROUTE * g + 1)
                nc.vector.tensor_tensor(score[:, :, :], logits, best, ALU.is_ge).then_inc(routed, 1)
                dve.wait_ge(routed, ROUTE * g + 2)
                nc.vector.tensor_tensor(score[:, :, :], score[:, :, :], order[:, :, :], ALU.mult).then_inc(routed, 1)
                dve.wait_ge(routed, ROUTE * g + 3)
                nc.vector.tensor_reduce(top[:, :], score[:, :, :], AX.X, ALU.max).then_inc(routed, 1)
                dve.wait_ge(routed, ROUTE * g + 4)
                dve.wait_ge(mask_done, START + 2 * g)
                nc.vector.tensor_tensor(mask[:, :, :], score[:, :, :], best, ALU.is_equal).then_inc(routed, 1)

            def mask_pixels(g, pair):
                for e in range(2):
                    if e == 0:
                        dve.wait_ge(mask_done, START + 2 * g + pair + 1)
                    dve.wait_ge(moe_done, START + (EXPERTS * g + 2 * pair + e - 1 if pair or e else EXPERTS * g))
                    nc.vector.tensor_tensor(xm[:, e, :, :], xn[:, :, :],
                                            p_mask[:, e:e + 1, :].to_broadcast([P, HALVES, PIX]),
                                            ALU.mult).then_inc(xm_ready, 1)

            def finish_output(q, j):
                g = COLS * q + j
                dve.wait_ge(moe_done, START + EXPERTS * (g + 1))
                at = x1[:, bass.ds(q % STRIP_RING, 1), :, :, PATCH * j:PATCH * (j + 1)].rearrange(
                    "p o h r c -> p (o h) r c")
                nc.vector.tensor_tensor(at, p_moe[:, :].rearrange("p (h r c) -> p h r c", h=HALVES, c=PATCH),
                                        at, ALU.add).then_inc(out_ready, 1)

            def x_stat(image, n):
                i, rest = divmod(n, HALVES * STRIP_PIX // STAT_PIX)
                h, c = divmod(rest, STRIP_PIX // STAT_PIX)
                dve.wait_ge(x_in[i], 16 * (image + 1))
                rows = STAT_PIX // SIDE
                at = 1 + PATCH * i + rows * c
                nc.vector.bn_stats(stat_x[:, h, STRIP_PIX // STAT_PIX * i + c, :],
                                   xin[:, h, at:at + rows, :].rearrange("p r c -> p (r c)")).then_inc(x_stats, 1)

            def gn_before(chain, stats):
                base = GN_OPS * chain
                for h in range(HALVES):
                    nc.vector.bn_aggr(mv[:, h, :], stats[:, h, :, :].rearrange("p n v -> p (n v)")).then_inc(gn_dve, 1)
                dve.wait_ge(gn_dve, base + 2)
                nc.vector.tensor_tensor(sq[:, :], mv[:, :, 0], mv[:, :, 0], ALU.mult).then_inc(gn_dve, 1)
                dve.wait_ge(gn_dve, base + 3)
                nc.vector.tensor_tensor(mv[:, :, 1], mv[:, :, 1], sq[:, :], ALU.add).then_inc(gn_dve, 1)

            def gn_middle(chain):
                base = GN_OPS * chain + GN_A
                dve.wait_ge(gn_sums, chain + 1)
                nc.vector.tensor_copy(gmv[:, :, :].rearrange("p h v -> p (h v)"), p_table[:, 0:2 * HALVES]).then_inc(gn_dve, 1)
                dve.wait_ge(gn_dve, base + 1)
                nc.vector.tensor_tensor(gsq[:, :], gmv[:, :, 0], gmv[:, :, 0], ALU.mult).then_inc(gn_dve, 1)
                dve.wait_ge(gn_dve, base + 2)
                nc.vector.tensor_tensor(gvar[:, :], gmv[:, :, 1], gsq[:, :], ALU.subtract).then_inc(gn_dve, 1)
                dve.wait_ge(gn_dve, base + 3)
                nc.vector.tensor_scalar(gvar[:, :], gvar[:, :], EPS, None, ALU.add).then_inc(gn_dve, 1)

            def gn_after(chain, scale, shift, below):
                base = GN_OPS * chain + GN_A + GN_B
                dve.wait_ge(gn_root, chain + 1)
                nc.vector.reciprocal(scale[:, :], root[:, :]).then_inc(gn_dve, 1)
                dve.wait_ge(gn_dve, base + 1)
                nc.vector.scalar_tensor_tensor(out=shift[:, :], in0=gmv[:, :, 0], scalar=-1.0, in1=scale[:, :],
                                               op0=ALU.mult, op1=ALU.mult).then_inc(gn_dve, 1)
                dve.wait_ge(gn_dve, base + 2)
                if below:
                    nc.vector.tensor_copy(shift_below[:, 0:STRIPS - 1, :],
                                          shift[:, :].rearrange("p (o h) -> p o h", o=1)
                                          .to_broadcast([P, STRIPS - 1, HALVES])).then_inc(gn_dve, 1)
                else:
                    nc.vector.tensor_copy(sq[:, :], shift[:, :]).then_inc(gn_dve, 1)

            def strip_body(i, step, s, last):
                for j in range(COLS):
                    for k in range(TAPS):
                        l = TAPS * j + k
                        if step.sample is not None and not (last and l + 2 >= PAIRS):
                            blend(STRIPS * step.sample + s, l + 2)
                        if step.table is not None and j == COLS - 1:
                            for op in range(2 * k, min(2 * k + 2, PREP)):
                                prepare(STRIPS * step.table + s, s, op)
                        if step.expert is not None:
                            q = STRIPS * step.expert + s
                            if k == 2:
                                route(COLS * q + j)
                            if k == 4 or k == 6:
                                mask_pixels(COLS * q + j, k // 2 - 2)
                            if k == 8:
                                finish_output(q, j)
                        if last and step.refill is not None:
                            if TAPS + 2 <= l < TAPS + 2 + 20:
                                for n in range(2 * (l - TAPS - 2), 2 * (l - TAPS - 2) + 2):
                                    x_stat(step.refill, n)
                            if l == TAPS * (COLS - 1) + 3:
                                dve.wait_ge(x_stats, HALVES * STAT_PIECES * (step.refill + 1))
                                gn_before(chain_of[i, "x"], stat_x)
                            if l == TAPS * (COLS - 1) + 5:
                                gn_middle(chain_of[i, "x"])
                            if l == TAPS * (COLS - 1) + 7:
                                gn_after(chain_of[i, "x"], scale_x, shift_x, True)
                        if step.sample is not None and k == TAPS - 1:
                            finish_patch(STRIPS * step.sample + s, s, j)

            for i, step in enumerate(STEPS):
                if step.sample is not None:
                    for l in range(2):
                        blend(STRIPS * step.sample, l)
                each_strip(dve, step, lambda s, last: strip_body(i, step, s, last))
                if step.only_refill:
                    dve.wait_ge(weights_in, 16 * 3)
                    nc.vector.tensor_tensor(
                        wexp[:, :, :].rearrange("p (e h) n -> p e (h n)", e=EXPERTS),
                        wexp[:, :, :].rearrange("p (e h) n -> p e (h n)", e=EXPERTS),
                        xm[:, 0:1, :, :].rearrange("p o h n -> p o (h n)").to_broadcast([P, EXPERTS, HALVES * CH]),
                        ALU.add).then_inc(consts_made, 1)
                if step.sample is not None:
                    dve.wait_ge(x1_stats, HALVES * COLS * STRIPS * (step.sample + 1))
                    gn_before(chain_of[i, "x1"], stat_x1)
                    gn_middle(chain_of[i, "x1"])
                    gn_after(chain_of[i, "x1"], scale_x1, shift_x1, False)


def kernel(x, L0_conv_w_off, L0_conv_w_deform, L1_conv_Wr, L1_conv_We, L1_conv_Ws):
    import numpy as np
    import concourse.bacc as bacc
    from concourse.bass_utils import run_bass_kernel_spmd

    p = np.arange(P)
    tile = np.arange(STRIP_TILES)[None, :, None]
    tap = np.arange(TAPS)[None, None, :]
    py = (tile % TILES) * 8 + p[:, None, None] // PATCH + tap // 3 - 1
    px = (tile // TILES) * PATCH + p[:, None, None] % PATCH + tap % 3 - 1
    position = np.stack([np.broadcast_to(a, (P, STRIP_TILES, TAPS)) for a in (py, px)], 1)
    position = position.reshape(P, 2, STRIP_TILES * TAPS).astype(np.float32)
    strip_row = np.broadcast_to(np.arange(STRIPS) * PATCH, (P, STRIPS)).astype(np.float32)
    ident = np.eye(P, dtype=np.float32)
    group_mean = np.kron(np.eye(P // GROUP), np.full((GROUP, GROUP), 1 / GROUP)).astype(np.float32)
    sum_parts = np.tile(np.eye(P // QUADS, OFFS), (QUADS, 1)).astype(np.float32)
    first_wins = np.broadcast_to(EXPERTS - np.arange(EXPERTS), (P, TILES, EXPERTS)).astype(np.float32)

    arrays = {
        "x_in": np.asarray(x).reshape(IMAGES, HALVES, P, SIDE * SIDE),
        "w_offset": np.asarray(L0_conv_w_off).reshape(OFFS, HALVES, P, TAPS).transpose(2, 3, 1, 0)
        .reshape(P, TAPS * HALVES, OFFS),
        "w_deform": np.asarray(L0_conv_w_deform).reshape(CH, HALVES, P, TAPS).transpose(2, 3, 1, 0)
        .reshape(P, TAPS * HALVES, CH),
        "w_router": np.asarray(L1_conv_Wr).reshape(HALVES, P, EXPERTS).transpose(1, 0, 2),
        "w_expert": np.asarray(L1_conv_We).reshape(EXPERTS, HALVES, P, CH).transpose(2, 0, 1, 3)
        .reshape(P, EXPERTS * HALVES, CH),
        "w_shared": np.asarray(L1_conv_Ws).reshape(HALVES, P, CH).transpose(1, 0, 2),
        "ident": ident, "group_mean": group_mean, "position": position,
        "strip_row": strip_row, "first_wins": first_wins, "sum_parts": sum_parts,
    }
    arrays = {name: np.ascontiguousarray(a) for name, a in arrays.items()}
    nc = bacc.Bacc("TRN2", target_bir_lowering=False, num_devices=1, dynamic_dma_scratch_size=4096)
    args = [nc.dram_tensor(f"{name}_dram", a.shape, mybir.dt.from_np(a.dtype), kind="ExternalInput").ap()
            for name, a in arrays.items()]
    out = nc.dram_tensor("out_dram", (IMAGES, HALVES, P, SIDE * SIDE), F32, kind="ExternalOutput").ap()
    build(nc, *args, out)
    r = run_bass_kernel_spmd(nc, [{f"{name}_dram": a for name, a in arrays.items()}], core_ids=[0])
    return r.results[0]["out_dram"].reshape(IMAGES, CH, SIDE, SIDE)
```

```python
from contextlib import ExitStack

import concourse.bass as bass
from concourse import mybir

F32 = mybir.dt.float32
BF16 = mybir.dt.bfloat16
I32 = mybir.dt.int32
U32 = mybir.dt.uint32
ALU = mybir.AluOpType
ACT = mybir.ActivationFunctionType
AX = mybir.AxisListType

P = 128
IMAGES, CH, SIDE = 4, 256, 80
HALVES = CH // P
TAPS = 9
PATCH = 16
STRIPS = SIDE // PATCH
COLS = SIDE // PATCH
TILES = 2
PIX = PATCH * PATCH
STRIP_PIX = PATCH * SIDE
STRIP_TILES = COLS * TILES
EXPERTS = 4
OFFS = 2 * TAPS
GROUP = 8

RIM = 2
WIDE = SIDE + 2 * RIM
ENTRIES = (SIDE + 2 * RIM - 1) * WIDE
TROW = 112
TURNS = WIDE * PATCH // TROW
CHUNK = 2
CHUNKS = TURNS // CHUNK

PAIRS = COLS * TAPS
UNITS = PAIRS * TILES
RING = 9
STRIP_RING = STRIPS + 1
QUADS = 4
PART_ROUNDS = -(-TAPS * HALVES // QUADS)
CHUNK_SLOTS = 6
PART_SLOTS = PART_ROUNDS + 2
STAT_PIX = 320
STAT_PIECES = SIDE * SIDE // STAT_PIX
PREP = 15
STAGE = 3 * HALVES
EPS = 1e-5
START = 1


class Step:

    def __init__(self, b):
        self.sample = b if 0 <= b < IMAGES else None
        self.table = b + 1 if 0 <= b + 1 < IMAGES else None
        self.refill = b + 2 if b + 2 < IMAGES else None
        self.expert = b - 1 if 0 <= b - 1 < IMAGES else None
        self.only_refill = b == -2


STEPS = [Step(b) for b in range(-2, IMAGES + 1)]


def each_strip(eng, step, body):
    if not step.only_refill:
        body(0, True, False)
        with eng.Fori(1, STRIPS - 1) as s:
            body(s, False, False)
    body(STRIPS - 1, False, True)


def gn_chains():
    at, n = {}, 0
    for i, step in enumerate(STEPS):
        if step.refill is not None:
            at[i, "x"] = n
            n += 1
        if step.sample is not None:
            at[i, "x1"] = n
            n += 1
    return at


GN_A, GN_B, GN_C = 4, 4, 3
GN_OPS = GN_A + GN_B + GN_C


def build(nc, x, w_offset, w_deform, w_router, w_expert, w_shared, ident, group_mean, position,
          strip_row, first_wins, sum_parts, out):
    chain_of = gn_chains()
    tables = [nc.dram_tensor(f"table{b}", [ENTRIES, 2 * CH], F32, kind="Internal") for b in range(IMAGES)]

    with ExitStack() as ctx:
        def sb(name, shape, dt=F32):
            return ctx.enter_context(nc.sbuf_tensor(name, shape, dt))

        def pb(name, shape):
            return ctx.enter_context(nc.psum_tensor(name, shape, F32))

        def sem(name):
            return ctx.enter_context(nc.semaphore(name))

        idn = sb("idn", [P, P])
        idn_bf = sb("idn_bf", [P, P], BF16)
        gmean = sb("gmean", [P, P])
        posc = sb("posc", [P, 2, STRIP_TILES * TAPS])
        srow = sb("srow", [P, STRIPS])
        order = sb("order", [P, TILES, EXPERTS])
        woff = sb("woff", [P, TAPS * HALVES, P // QUADS])
        pick = sb("pick", [P, OFFS])
        wdef = sb("wdef", [P, TAPS * HALVES, CH])
        wrt = sb("wrt", [P, HALVES, EXPERTS])
        wexp = sb("wexp", [P, EXPERTS * HALVES, CH])
        xin = sb("xin", [P, HALVES, SIDE + 2, SIDE])
        strip = sb("strip", [P, HALVES, PATCH + 2, WIDE])
        turned = sb("turned", [TROW, 2, CHUNK, CH])
        stat_x = sb("stat_x", [P, HALVES, STAT_PIECES, 6])
        part = sb("part", [P, PIX])
        pyx = sb("pyx", [P, 2, STRIP_TILES * TAPS])
        whole = sb("whole", [P, 2, STRIP_TILES * TAPS], I32)
        floor = sb("floor", [P, 2, STRIP_TILES * TAPS])
        tmp = whole[:, :, :].bitcast(F32)
        w_far = pyx
        w_near = floor
        entry_img = sb("entry_img", [P, STRIPS * STRIP_TILES, TAPS], U32)
        weight_img = sb("weight_img", [P, STRIPS * STRIP_TILES, TAPS, 4])
        entry = [sb(f"entry{j}", [P, TILES, TAPS], U32) for j in range(COLS)]
        weight = [sb(f"weight{j}", [P, TILES, TAPS, 4]) for j in range(COLS)]
        corners = sb("corners", [P, RING, 4 * CH])
        val = sb("val", [P, 2, HALVES, PIX])
        x1 = sb("x1", [P, STRIP_RING, HALVES, PATCH, SIDE])
        stat_x1 = sb("stat_x1", [P, HALVES, STRIPS * COLS, 6])
        xn = sb("xn", [P, HALVES, PIX])
        xm = sb("xm", [P, 2, HALVES, PIX])
        top = sb("top", [P, TILES])
        score = sb("score", [P, TILES, EXPERTS])
        mask = sb("mask", [P, TILES, EXPERTS], BF16)
        mv = sb("mv", [P, HALVES, 2])
        sq = sb("sq", [P, HALVES])
        gmv = sb("gmv", [P, HALVES, 2])
        gsq = sq
        gvar = sb("gvar", [P, HALVES])
        root = gvar
        affine = sb("affine", [P, 4, HALVES])
        scale_x, shift_x, scale_x1, shift_x1 = (affine[:, n, :] for n in range(4))
        shift_below = sb("shift_below", [P, STRIPS, HALVES])
        zero = sb("zero", [P, 1])

        p_turn = [pb(f"p_turn{i}", [P, HALVES * PIX]) for i in range(2)]
        p_acc = [pb(f"p_acc{i}", [P, HALVES * PIX]) for i in range(2)]
        p_part = pb("p_part", [P, PIX + STRIP_TILES * OFFS])
        p_offs = p_part[:, PIX:PIX + STRIP_TILES * OFFS]
        p_table = pb("p_table", [P, CHUNK, CH])
        p_route = pb("p_route", [P, 512])
        p_logits = p_route[:, 0:TILES * EXPERTS]
        p_mask = p_route[:, P:512].bitcast(BF16).rearrange("p (e n) -> p e n", e=EXPERTS - 1)
        p_moe = pb("p_moe", [P, HALVES * PIX])

        consts_in = sem("consts_in")
        weights_in = sem("weights_in")
        zeroed = sem("zeroed")
        consts_made = sem("consts_made")
        rim_out = sem("rim_out")
        x_in = [sem(f"x_in{i}") for i in range(STRIPS)]
        x_stats = sem("x_stats")
        gn_dve = sem("gn_dve")
        gn_sums = sem("gn_sums")
        gn_root = sem("gn_root")
        staged = sem("staged")
        part_done = sem("part_done")
        part_copied = sem("part_copied")
        offs_done = sem("offs_done")
        table_turned = sem("table_turned")
        table_copied = sem("table_copied")
        table_out = [sem(f"table_out{i}") for i in range(2)]
        prepped = sem("prepped")
        picked = sem("picked")
        gathered = [sem(f"gathered{i}") for i in range(RING)]
        unit_free = sem("unit_free")
        unit_taken = sem("unit_taken")
        scaled = sem("scaled")
        blended = sem("blended")
        val_ready = sem("val_ready")
        conv_done = sem("conv_done")
        resid_in = sem("resid_in")
        x1_done = sem("x1_done")
        x1_stats = sem("x1_stats")
        xn_ready = sem("xn_ready")
        logits_done = sem("logits_done")
        routed = sem("routed")
        mask_done = sem("mask_done")
        xm_ready = sem("xm_ready")
        moe_done = sem("moe_done")
        out_ready = sem("out_ready")
        out_stored = sem("out_stored")

        ROUTE = 5
        ZEROED = 6
        CONSTS = 8

        started = {
            "sync": [(table_out[0], 16), (table_out[1], 16), (out_stored, 16)],
            "scalar": [(val_ready, 1), (part_copied, 1), (table_copied, 1)],
            "tensor": [(conv_done, 1), (mask_done, 1), (moe_done, 1)],
            "vector": [(x1_done, 1), (xm_ready, 1), (out_ready, 1), (prepped, 1)],
        }

        def start(eng, name):
            for counter, unit in started[name]:
                eng.sem_inc(counter, START * unit)

        def reuse(n, l):
            return n if isinstance(l, int) and l == 0 else n - 1

        block = ctx.enter_context(nc.Block())

        @block.sync
        def _(sp):
            start(sp, "sync")
            sp.dma_start(idn[:, :], ident).then_inc(consts_in, 16)
            sp.dma_start(gmean[:, :], group_mean).then_inc(consts_in, 16)
            sp.dma_start(posc[:, :, :], position).then_inc(consts_in, 16)
            sp.dma_start(srow[:, :], strip_row).then_inc(consts_in, 16)
            sp.dma_start(order[:, :, :], first_wins).then_inc(consts_in, 16)
            sp.dma_start(wrt[:, :, :], w_router).then_inc(consts_in, 16)
            sp.dma_start(pick[:, :], sum_parts).then_inc(consts_in, 16)
            sp.wait_ge(zeroed, ZEROED)
            sp.dma_start(woff[:, :, 0:OFFS], w_offset).then_inc(consts_in, 16)

            def load_x(image, i):
                sp.dma_start(xin[:, :, 1 + PATCH * i:1 + PATCH * (i + 1), :].rearrange("p h r c -> p h (r c)"),
                             x[image, :, :, STRIP_PIX * i:STRIP_PIX * (i + 1)].rearrange("h p n -> p h n")
                             ).then_inc(x_in[i], 16)

            def rims():
                zeros = strip[0:WIDE, 0, :, :].rearrange("p r c -> p (r c)")
                for t in tables:
                    last = ENTRIES - WIDE
                    sp.dma_start(t[0:WIDE, :], zeros[:, 0:2 * CH]).then_inc(rim_out, 16)
                    sp.dma_start(t[WIDE:2 * WIDE, 0:CH], zeros[:, 0:CH]).then_inc(rim_out, 16)
                    sp.dma_start(t[last - WIDE:last, CH:2 * CH], zeros[:, 0:CH]).then_inc(rim_out, 16)
                    sp.dma_start(t[last:ENTRIES, :], zeros[:, 0:2 * CH]).then_inc(rim_out, 16)

            def strip_body(step, s, last):
                if step.sample is not None:
                    q = STRIPS * step.sample + s
                    if step.expert is not None:
                        sp.wait_ge(out_stored, 16 * START + (q - STRIPS) * 16)
                    sp.dma_start(x1[:, bass.ds(q % STRIP_RING, 1), :, :, :].rearrange("p o h r c -> p (o h) (r c)"),
                                 x[step.sample, :, :, bass.ds(STRIP_PIX * s, STRIP_PIX)].rearrange("h p n -> p h n")
                                 ).then_inc(resid_in, 16)
                if last and step.refill is not None:
                    if step.table is not None:
                        sp.wait_ge(staged, STAGE * STRIPS * (step.table + 1))
                    for i in range(STRIPS):
                        if step.sample is not None:
                            sp.wait_ge(conv_done, START + PAIRS * (STRIPS * step.sample + s) + 2 * i + 1)
                        load_x(step.refill, i)
                if step.table is not None:
                    t = tables[step.table]
                    for c in range(CHUNKS):
                        sp.wait_ge(table_copied, START + CHUNKS * (STRIPS * step.table + s) + c + 1)
                        f = (PATCH * s + RIM) * WIDE + TROW * CHUNK * c
                        src = turned[:, c % 2, :, :]
                        sp.dma_start(t[bass.ds(f, TROW * CHUNK), 0:CH].rearrange("(i p) c -> p i c", p=TROW),
                                     src).then_inc(table_out[c % 2], 16)
                        sp.dma_start(t[bass.ds(f - WIDE, TROW * CHUNK), CH:2 * CH].rearrange("(i p) c -> p i c", p=TROW),
                                     src).then_inc(table_out[c % 2], 16)
                if step.expert is not None:
                    q = STRIPS * step.expert + s
                    sp.wait_ge(out_ready, START + COLS * (q + 1))
                    sp.dma_start(out[step.expert, :, :, bass.ds(STRIP_PIX * s, STRIP_PIX)].rearrange("h p n -> p h n"),
                                 x1[:, bass.ds(q % STRIP_RING, 1), :, :, :].rearrange("p o h r c -> p (o h) (r c)")
                                 ).then_inc(out_stored, 16)

            for i, step in enumerate(STEPS):
                each_strip(sp, step, lambda s, first, last: strip_body(step, s, last))
                if step.only_refill:
                    rims()
                    sp.dma_start(wdef[:, :, :], w_deform).then_inc(weights_in, 16)
                    sp.dma_start(wexp[:, :, :], w_expert).then_inc(weights_in, 16)
                    sp.dma_start(xm[:, 0, :, :], w_shared).then_inc(weights_in, 16)
            sp.wait_ge(out_stored, 16 * START + 16 * STRIPS * IMAGES)

        @block.gpsimd
        def _(pool):
            nc.gpsimd.memset(strip[:, :, :, :], 0.0).then_inc(zeroed, 1)
            nc.gpsimd.memset(xin[:, :, 0:1, :], 0.0).then_inc(zeroed, 1)
            nc.gpsimd.memset(xin[:, :, SIDE + 1:SIDE + 2, :], 0.0).then_inc(zeroed, 1)
            nc.gpsimd.memset(shift_below[:, :, :], 0.0).then_inc(zeroed, 1)
            nc.gpsimd.memset(zero[:, :], 0.0).then_inc(zeroed, 1)
            nc.gpsimd.memset(woff[:, :, :], 0.0).then_inc(zeroed, 1)
            nc.gpsimd.memset(corners[:, 0, 0:1], 0.0).then_inc(unit_free, RING)
            pool.wait_ge(unit_free, RING)

            def strip_body(step, s, last):
                q = STRIPS * step.sample + s
                for j in range(COLS):
                    g = COLS * q + j
                    tile = STRIP_TILES * s + TILES * j
                    nc.gpsimd.tensor_copy(entry[j][:, :, :], entry_img[:, bass.ds(tile, TILES), :]).then_inc(picked, 1)
                    nc.gpsimd.tensor_copy(weight[j][:, :, :, :].rearrange("p t k c -> p t (k c)"),
                                          weight_img[:, bass.ds(tile, TILES), :, :].rearrange("p t k c -> p t (k c)")
                                          ).then_inc(picked, 1)
                    pool.wait_ge(picked, 2 * (g + 1))
                    for v in range(UNITS // COLS):
                        k, t = divmod(v, TILES)
                        local = UNITS // COLS * j + v
                        pool.wait_ge(unit_free, UNITS * q + local + 1).then_inc(unit_taken, 1)
                        nc.gpsimd.indirect_dma_start(
                            corners[:, local % RING, :], None, tables[step.sample][:, :],
                            bass.IndirectOffsetOnAxis(ap=entry[j][:, t, k:k + 1], axis=0),
                        ).then_inc(gathered[local % RING], 16)

            for step in STEPS:
                if step.sample is not None:
                    pool.wait_ge(prepped, START + PREP * STRIPS * (step.sample + 1))
                    pool.wait_ge(rim_out, 16 * 4 * IMAGES)
                    for half in range(2):
                        pool.wait_ge(table_out[half], 16 * START + 16 * CHUNKS * STRIPS * (step.sample + 1))
                    each_strip(pool, step, lambda s, first, last: strip_body(step, s, last))

        @block.scalar
        def _(act):
            start(act, "scalar")
            act.wait_ge(zeroed, ZEROED)

            def scale_corner(q, l):
                j, k = divmod(l % PAIRS, TAPS)
                for t in range(TILES):
                    local = TILES * (l % PAIRS) + t
                    act.wait_ge(gathered[local % RING], 16 * (UNITS // RING * (q + l // PAIRS) + local // RING + 1))
                    c = corners[:, local % RING, 0:CH]
                    nc.scalar.activation(c, c, ACT.Identity, bias=zero[:, 0:1],
                                         scale=weight[j][:, t, k, 0:1]).then_inc(scaled, 1)

            def copy_val(q, l):
                n = PAIRS * q + l
                act.wait_ge(unit_free, RING + TILES * (n + 1))
                act.wait_ge(conv_done, START + reuse(n, l % PAIRS))
                b = l % PAIRS % 2
                nc.scalar.activation(val[:, b, :, :].rearrange("p h n -> p (h n)"), p_turn[b][:, :],
                                     ACT.Copy).then_inc(val_ready, 1)

            def stage(s, piece, edge_row):
                h, piece = divmod(piece, 3)
                sc = scale_x[:, h:h + 1]
                cols = slice(RIM, RIM + SIDE)
                if piece == 0:
                    nc.scalar.activation(strip[:, h, 1:1 + PATCH, cols], xin[:, h, bass.ds(PATCH * s + 1, PATCH), :],
                                         ACT.Identity, bias=shift_x[:, h:h + 1], scale=sc).then_inc(staged, 1)
                elif piece == 1:
                    bias = zero[:, 0:1] if edge_row else shift_x[:, h:h + 1]
                    nc.scalar.activation(strip[:, h, 0:1, cols], xin[:, h, bass.ds(PATCH * s, 1), :],
                                         ACT.Identity, bias=bias, scale=sc).then_inc(staged, 1)
                else:
                    nc.scalar.activation(strip[:, h, 1 + PATCH:2 + PATCH, cols],
                                         xin[:, h, bass.ds(PATCH * (s + 1) + 1, 1), :], ACT.Identity,
                                         bias=shift_below[:, bass.ds(s, 1), h], scale=sc).then_inc(staged, 1)

            def normalize_patch(q, j):
                g = COLS * q + j
                q, j = q + j // COLS, j % COLS
                act.wait_ge(xm_ready, START + (EXPERTS - 1) * g)
                if not (isinstance(g, int) and g == 0):
                    act.wait_ge(moe_done, START + EXPERTS * (g - 1) + 1)
                for h in range(HALVES):
                    nc.scalar.activation(
                        xn[:, h, :].rearrange("p (r c) -> p r c", c=PATCH),
                        x1[:, bass.ds(q % STRIP_RING, 1), h, :, PATCH * j:PATCH * (j + 1)]
                        .rearrange("p o r c -> p (o r) c"),
                        ACT.Identity, bias=shift_x1[:, h:h + 1], scale=scale_x1[:, h:h + 1]
                    ).then_inc(xn_ready, 1)

            def gn_take_root(chain):
                act.wait_ge(gn_dve, GN_OPS * chain + GN_A + GN_B)
                nc.scalar.activation(root[:, :], gvar[:, :], ACT.Sqrt).then_inc(gn_root, 1)

            def strip_body(i, step, s, last):
                for j in range(COLS):
                    for k in range(TAPS):
                        l = TAPS * j + k
                        if step.sample is not None:
                            q = STRIPS * step.sample + s
                            if not (last and l + 3 >= PAIRS):
                                scale_corner(q, l + 3)
                            if not (last and l + 1 >= PAIRS):
                                copy_val(q, l + 1)
                        if step.table is not None and l < CHUNK_SLOTS * CHUNKS and l % CHUNK_SLOTS == 1:
                            c = l // CHUNK_SLOTS
                            q = STRIPS * step.table + s
                            act.wait_ge(table_turned, CHUNKS * q + c + 1)
                            act.wait_ge(table_out[c % 2], 16 * START + 16 * 2 * (CHUNKS // 2 * q + c // 2))
                            nc.scalar.activation(turned[:, c % 2, :, :], p_table[0:TROW, :, :],
                                                 ACT.Copy).then_inc(table_copied, 1)
                        if step.table is not None and l < PART_SLOTS * COLS and l % PART_SLOTS == PART_ROUNDS:
                            g = COLS * (STRIPS * step.table + s) + l // PART_SLOTS
                            act.wait_ge(part_done, g + 1)
                            nc.scalar.activation(part[:, :], p_part[:, 0:PIX], ACT.Copy).then_inc(part_copied, 1)
                        if step.expert is not None and k == 6 and not (last and j == COLS - 1):
                            normalize_patch(STRIPS * step.expert + s, j + 1)
                        if j == COLS - 1:
                            if last and step.refill is not None:
                                if k == 5:
                                    gn_take_root(chain_of[i, "x"])
                                if k == 8:
                                    act.wait_ge(gn_dve, GN_OPS * (chain_of[i, "x"] + 1))
                                    if step.table is not None:
                                        act.wait_ge(offs_done, STRIPS * (step.table + 1))
                                    else:
                                        act.wait_ge(rim_out, 16 * 4 * IMAGES)
                                    for piece in range(STAGE):
                                        stage(0, piece, True)
                            elif not last and step.table is not None and 2 <= k < 2 + STAGE:
                                act.wait_ge(offs_done, STRIPS * step.table + s + 1)
                                stage(s + 1, k - 2, False)

            for i, step in enumerate(STEPS):
                if step.expert is not None:
                    act.wait_ge(gn_dve, GN_OPS * (chain_of[i - 1, "x1"] + 1))
                    normalize_patch(STRIPS * step.expert, 0)
                if step.sample is not None:
                    for l in range(3):
                        scale_corner(STRIPS * step.sample, l)
                    copy_val(STRIPS * step.sample, 0)
                each_strip(act, step, lambda s, first, last: strip_body(i, step, s, last))
                if step.sample is not None:
                    gn_take_root(chain_of[i, "x1"])

        @block.tensor
        def _(pe):
            start(pe, "tensor")
            pe.wait_ge(consts_in, 16 * CONSTS)

            def turn_pair(q, l):
                n = PAIRS * q + l
                l = l % PAIRS
                pe.wait_ge(val_ready, START + reuse(n, l))
                for t in range(TILES):
                    pe.wait_ge(blended, 6 * n + 5 + t)
                    unit = (TILES * l + t) % RING
                    for h in range(HALVES):
                        mm = nc.tensor.transpose(p_turn[l % 2][:, PIX * h + P * t:PIX * h + P * (t + 1)],
                                                 corners[:, unit, P * h:P * (h + 1)], idn[:, :])
                    mm.then_inc(unit_free, 1)

            def conv_pair(q, l):
                j, k = divmod(l, TAPS)
                n = PAIRS * q + l
                pe.wait_ge(val_ready, START + n + 1)
                if k == 0:
                    pe.wait_ge(x1_done, START + COLS * q + (j if j == 0 else j - 1))
                for m in range(HALVES):
                    for h in range(HALVES):
                        mm = nc.tensor.matmul(p_acc[j % 2][:, PIX * m:PIX * (m + 1)],
                                              wdef[:, HALVES * k + h, P * m:P * (m + 1)], val[:, l % 2, h, :],
                                              start=(k == 0 and h == 0 and m == 0), stop=(k == TAPS - 1),
                                              skip_group_check=True)
                mm.then_inc(conv_done, 1)

            def offset_part(q, l):
                j, i = divmod(l, PART_SLOTS)
                g = COLS * q + j
                if i < PART_ROUNDS:
                    if i == 0:
                        pe.wait_ge(part_copied, START + g)
                    for kh in range(QUADS * i, min(QUADS * (i + 1), TAPS * HALVES)):
                        k, h = divmod(kh, HALVES)
                        c = P // QUADS * (kh % QUADS)
                        row, col = k // 3, PATCH * j + k % 3 + RIM - 1
                        mm = nc.tensor.matmul(p_part[c:c + P // QUADS, 0:PIX], woff[:, kh, :],
                                              strip[:, h, row:row + PATCH, col:col + PATCH],
                                              start=(i == 0), stop=(kh + QUADS >= TAPS * HALVES))
                    if i == PART_ROUNDS - 1:
                        mm.then_inc(part_done, 1)
                elif i == PART_ROUNDS + 1:
                    pe.wait_ge(part_copied, START + g + 1)
                    for t in range(TILES):
                        at = OFFS * (TILES * j + t)
                        mm = nc.tensor.matmul(p_offs[:, at:at + OFFS], part[:, P * t:P * (t + 1)], pick[:, :],
                                              start=True, stop=True)
                    if j == COLS - 1:
                        mm.then_inc(offs_done, 1)

            def table_turn(q, c):
                pe.wait_ge(table_copied, START + CHUNKS * q + c)
                for i in range(CHUNK):
                    for h in range(HALVES):
                        rows = strip[:, h, :, :].rearrange("p r c -> p (r c)")
                        at = WIDE + TROW * (CHUNK * c + i)
                        mm = nc.tensor.transpose(p_table[0:TROW, i, P * h:P * (h + 1)],
                                                 rows[:, at:at + TROW], idn[:, :])
                mm.then_inc(table_turned, 1)

            def gn_group_sums(chain, tables_done):
                pe.wait_ge(gn_dve, GN_OPS * chain + GN_A)
                pe.wait_ge(table_copied, START + tables_done)
                nc.tensor.matmul(p_table[:, 0, 0:2 * HALVES], gmean[:, :],
                                 mv[:, :, :].rearrange("p h v -> p (h v)"), start=True, stop=True
                                 ).then_inc(gn_sums, 1)

            def logits(g):
                pe.wait_ge(xn_ready, HALVES * (g + 1))
                for t in range(TILES):
                    for h in range(HALVES):
                        mm = nc.tensor.matmul(p_logits[:, EXPERTS * t:EXPERTS * (t + 1)], xn[:, h, P * t:P * (t + 1)],
                                              wrt[:, h, :], start=(h == 0), stop=(h == HALVES - 1))
                mm.then_inc(logits_done, 1)

            def spread_masks(g):
                pe.wait_ge(routed, ROUTE * (g + 1))
                for e in range(1, EXPERTS):
                    for t in range(TILES):
                        mm = nc.tensor.transpose(p_mask[:, e - 1, P * t:P * (t + 1)],
                                                 mask[:, t, e:e + 1].to_broadcast([P, P]), idn_bf[:, :])
                mm.then_inc(mask_done, 1)

            def expert_products(g, e):
                if e == 0:
                    pe.wait_ge(xn_ready, HALVES * (g + 1))
                    pe.wait_ge(out_ready, START + g)
                else:
                    pe.wait_ge(xm_ready, START + (EXPERTS - 1) * g + e)
                for m in range(HALVES):
                    for h in range(HALVES):
                        pixels = xm[:, (e - 1) % 2, h, :] if e else xn[:, h, :]
                        mm = nc.tensor.matmul(p_moe[:, PIX * m:PIX * (m + 1)],
                                              wexp[:, HALVES * e + h, P * m:P * (m + 1)], pixels,
                                              start=(e == 0 and h == 0 and m == 0), stop=(e == EXPERTS - 1),
                                              skip_group_check=True)
                mm.then_inc(moe_done, 1)

            def expert_part(q, j, k, last):
                g = COLS * q + j
                if k == 0:
                    expert_products(g, 0)
                if k == 1:
                    spread_masks(g)
                if k == 3:
                    expert_products(g, 1)
                if k == 5:
                    expert_products(g, 2)
                if k == 7:
                    if not (last and j == COLS - 1):
                        logits(g + 1)
                    expert_products(g, 3)

            def strip_body(i, step, s, last):
                if step.table is not None:
                    q = STRIPS * step.table + s
                    pe.wait_ge(staged, STAGE * (q + 1))
                    pe.wait_ge(prepped, START + PREP * q)
                for j in range(COLS):
                    for k in range(TAPS):
                        l = TAPS * j + k
                        if step.sample is not None:
                            q = STRIPS * step.sample + s
                            if not (last and l + 1 >= PAIRS):
                                turn_pair(q, l + 1)
                            conv_pair(q, l)
                        if step.table is not None and j < COLS - 1:
                            q = STRIPS * step.table + s
                            if l % CHUNK_SLOTS == 0:
                                table_turn(q, l // CHUNK_SLOTS)
                            if l < PART_SLOTS * COLS:
                                offset_part(q, l)
                        if step.expert is not None:
                            expert_part(STRIPS * step.expert + s, j, k, last)
                        if last and step.refill is not None and l == TAPS * (COLS - 1) + 4:
                            done = 0 if step.table is None else CHUNKS * STRIPS * (step.table + 1)
                            gn_group_sums(chain_of[i, "x"], done)

            for i, step in enumerate(STEPS):
                if step.sample is not None:
                    if step.sample == 0:
                        pe.wait_ge(weights_in, 16 * 3)
                        pe.wait_ge(consts_made, 3)
                    turn_pair(STRIPS * step.sample, 0)
                if step.expert is not None:
                    logits(COLS * STRIPS * step.expert)
                each_strip(pe, step, lambda s, first, last: strip_body(i, step, s, last))
                if step.sample is not None:
                    tables_done = CHUNKS * STRIPS * min(step.sample + 2, IMAGES)
                    gn_group_sums(chain_of[i, "x1"], tables_done)

        @block.vector
        def _(dve):
            start(dve, "vector")
            dve.wait_ge(consts_in, 16 * CONSTS)
            nc.vector.tensor_copy(idn_bf[:, :], idn[:, :]).then_inc(consts_made, 1)

            def blend(q, l):
                n = PAIRS * q + l
                l = l % PAIRS
                j, k = divmod(l, TAPS)
                for c in range(1, 4):
                    for t in range(TILES):
                        unit = (TILES * l + t) % RING
                        if c == 1:
                            dve.wait_ge(scaled, TILES * n + t + 1)
                        else:
                            dve.wait_ge(blended, 6 * n + 2 * (c - 2) + t + 1)
                        acc = corners[:, unit, 0:CH]
                        nc.vector.scalar_tensor_tensor(
                            out=acc, in0=corners[:, unit, CH * c:CH * (c + 1)], scalar=weight[j][:, t, k, c:c + 1],
                            in1=acc, op0=ALU.mult, op1=ALU.add).then_inc(blended, 1)

            def finish_patch(q, s, j):
                g = COLS * q + j
                dve.wait_ge(conv_done, START + TAPS * (g + 1))
                if j == 0:
                    dve.wait_ge(resid_in, 16 * (q + 1))
                at = x1[:, bass.ds(q % STRIP_RING, 1), :, :, PATCH * j:PATCH * (j + 1)].rearrange(
                    "p o h r c -> p (o h) r c")
                nc.vector.tensor_tensor(at, p_acc[j % 2][:, :].rearrange("p (h r c) -> p h r c", h=HALVES, c=PATCH),
                                        at, ALU.add).then_inc(x1_done, 1)
                dve.wait_ge(x1_done, START + g + 1)
                for h in range(HALVES):
                    nc.vector.bn_stats(stat_x1[:, h, bass.ds(COLS * s + j, 1), :],
                                       x1[:, bass.ds(q % STRIP_RING, 1), h, :, PATCH * j:PATCH * (j + 1)]
                                       .rearrange("p o r c -> p (o r) c")).then_inc(x1_stats, 1)

            def prepare(q, s, op):
                offs = p_offs.rearrange("p (n v) -> p v n", v=2)
                row = bass.ds(STRIP_TILES * s, STRIP_TILES)
                if op == 0:
                    dve.wait_ge(offs_done, q + 1)
                elif op != 1:
                    dve.wait_ge(prepped, START + PREP * q + op)
                if op == 0:
                    ins = nc.vector.scalar_tensor_tensor(out=pyx[:, 0, :], in0=posc[:, 0, :], scalar=srow[:, bass.ds(s, 1)],
                                                         in1=offs[:, 0, :], op0=ALU.add, op1=ALU.add)
                elif op == 1:
                    ins = nc.vector.tensor_tensor(pyx[:, 1, :], posc[:, 1, :], offs[:, 1, :], ALU.add)
                elif op == 2:
                    ins = nc.vector.tensor_scalar(pyx[:, :, :], pyx[:, :, :], float(-RIM), SIDE + 0.5, ALU.max, ALU.min)
                elif op == 3:
                    ins = nc.vector.tensor_copy(whole[:, :, :], pyx[:, :, :])
                elif op == 4:
                    ins = nc.vector.tensor_copy(floor[:, :, :], whole[:, :, :])
                elif op == 5:
                    ins = nc.vector.tensor_tensor(tmp[:, :, :], floor[:, :, :], pyx[:, :, :], ALU.is_gt)
                elif op == 6:
                    ins = nc.vector.tensor_tensor(floor[:, :, :], floor[:, :, :], tmp[:, :, :], ALU.subtract)
                elif op == 7:
                    ins = nc.vector.tensor_tensor(w_far[:, :, :], pyx[:, :, :], floor[:, :, :], ALU.subtract)
                elif op == 8:
                    ins = nc.vector.scalar_tensor_tensor(out=tmp[:, 0, :], in0=floor[:, 0, :], scalar=float(WIDE),
                                                         in1=floor[:, 1, :], op0=ALU.mult, op1=ALU.add)
                elif op == 9:
                    ins = nc.vector.tensor_scalar(entry_img[:, row, :].rearrange("p t k -> p (t k)"), tmp[:, 0, :],
                                                  float(RIM * WIDE + RIM), None, ALU.add)
                elif op == 10:
                    ins = nc.vector.tensor_scalar(w_near[:, :, :], w_far[:, :, :], -1.0, 1.0, ALU.mult, ALU.add)
                else:
                    c = op - 11
                    wy = w_far if c % 2 else w_near
                    wx = w_far if c // 2 else w_near
                    ins = nc.vector.tensor_tensor(weight_img[:, row, :, c].rearrange("p t k -> p (t k)"),
                                                  wy[:, 0, :], wx[:, 1, :], ALU.mult)
                ins.then_inc(prepped, 1)

            def route(g):
                logits = p_logits.rearrange("p (t e) -> p t e", e=EXPERTS)
                best = top[:, :].rearrange("p (t o) -> p t o", o=1).to_broadcast([P, TILES, EXPERTS])
                dve.wait_ge(logits_done, g + 1)
                nc.vector.tensor_reduce(top[:, :], logits, AX.X, ALU.max).then_inc(routed, 1)
                dve.wait_ge(routed, ROUTE * g + 1)
                nc.vector.tensor_tensor(score[:, :, :], logits, best, ALU.is_ge).then_inc(routed, 1)
                dve.wait_ge(routed, ROUTE * g + 2)
                nc.vector.tensor_tensor(score[:, :, :], score[:, :, :], order[:, :, :], ALU.mult).then_inc(routed, 1)
                dve.wait_ge(routed, ROUTE * g + 3)
                nc.vector.tensor_reduce(top[:, :], score[:, :, :], AX.X, ALU.max).then_inc(routed, 1)
                dve.wait_ge(routed, ROUTE * g + 4)
                dve.wait_ge(mask_done, START + g)
                nc.vector.tensor_tensor(mask[:, :, :], score[:, :, :], best, ALU.is_equal).then_inc(routed, 1)

            def mask_pixels(g, e):
                dve.wait_ge(mask_done, START + g + 1)
                dve.wait_ge(moe_done, START + EXPERTS * g + (2 if e == 3 else 0))
                nc.vector.tensor_tensor(xm[:, (e - 1) % 2, :, :], xn[:, :, :],
                                        p_mask[:, e - 1:e, :].to_broadcast([P, HALVES, PIX]),
                                        ALU.mult).then_inc(xm_ready, 1)

            def finish_output(q, j):
                g = COLS * q + j
                dve.wait_ge(moe_done, START + EXPERTS * (g + 1))
                at = x1[:, bass.ds(q % STRIP_RING, 1), :, :, PATCH * j:PATCH * (j + 1)].rearrange(
                    "p o h r c -> p (o h) r c")
                nc.vector.tensor_tensor(at, p_moe[:, :].rearrange("p (h r c) -> p h r c", h=HALVES, c=PATCH),
                                        at, ALU.add).then_inc(out_ready, 1)

            def x_stat(image, n):
                i, rest = divmod(n, HALVES * STRIP_PIX // STAT_PIX)
                h, c = divmod(rest, STRIP_PIX // STAT_PIX)
                dve.wait_ge(x_in[i], 16 * (image + 1))
                rows = STAT_PIX // SIDE
                at = 1 + PATCH * i + rows * c
                nc.vector.bn_stats(stat_x[:, h, STRIP_PIX // STAT_PIX * i + c, :],
                                   xin[:, h, at:at + rows, :].rearrange("p r c -> p (r c)")).then_inc(x_stats, 1)

            def gn_before(chain, stats):
                base = GN_OPS * chain
                for h in range(HALVES):
                    nc.vector.bn_aggr(mv[:, h, :], stats[:, h, :, :].rearrange("p n v -> p (n v)")).then_inc(gn_dve, 1)
                dve.wait_ge(gn_dve, base + 2)
                nc.vector.tensor_tensor(sq[:, :], mv[:, :, 0], mv[:, :, 0], ALU.mult).then_inc(gn_dve, 1)
                dve.wait_ge(gn_dve, base + 3)
                nc.vector.tensor_tensor(mv[:, :, 1], mv[:, :, 1], sq[:, :], ALU.add).then_inc(gn_dve, 1)

            def gn_middle(chain):
                base = GN_OPS * chain + GN_A
                dve.wait_ge(gn_sums, chain + 1)
                nc.vector.tensor_copy(gmv[:, :, :].rearrange("p h v -> p (h v)"), p_table[:, 0, 0:2 * HALVES]).then_inc(gn_dve, 1)
                dve.wait_ge(gn_dve, base + 1)
                nc.vector.tensor_tensor(gsq[:, :], gmv[:, :, 0], gmv[:, :, 0], ALU.mult).then_inc(gn_dve, 1)
                dve.wait_ge(gn_dve, base + 2)
                nc.vector.tensor_tensor(gvar[:, :], gmv[:, :, 1], gsq[:, :], ALU.subtract).then_inc(gn_dve, 1)
                dve.wait_ge(gn_dve, base + 3)
                nc.vector.tensor_scalar(gvar[:, :], gvar[:, :], EPS, None, ALU.add).then_inc(gn_dve, 1)

            def gn_after(chain, scale, shift, below):
                base = GN_OPS * chain + GN_A + GN_B
                dve.wait_ge(gn_root, chain + 1)
                nc.vector.reciprocal(scale[:, :], root[:, :]).then_inc(gn_dve, 1)
                dve.wait_ge(gn_dve, base + 1)
                nc.vector.scalar_tensor_tensor(out=shift[:, :], in0=gmv[:, :, 0], scalar=-1.0, in1=scale[:, :],
                                               op0=ALU.mult, op1=ALU.mult).then_inc(gn_dve, 1)
                dve.wait_ge(gn_dve, base + 2)
                if below:
                    nc.vector.tensor_copy(shift_below[:, 0:STRIPS - 1, :],
                                          shift[:, :].rearrange("p (o h) -> p o h", o=1)
                                          .to_broadcast([P, STRIPS - 1, HALVES])).then_inc(gn_dve, 1)
                else:
                    nc.vector.tensor_copy(sq[:, :], shift[:, :]).then_inc(gn_dve, 1)

            def strip_body(i, step, s, first, last):
                for j in range(COLS):
                    for k in range(TAPS):
                        l = TAPS * j + k
                        if step.sample is not None and l == 0 and not first:
                            finish_patch(STRIPS * step.sample + s - 1, s - 1, COLS - 1)
                        if step.sample is not None and not (last and l + 2 >= PAIRS):
                            blend(STRIPS * step.sample + s, l + 2)
                        if step.table is not None and j == COLS - 1:
                            for op in range(2 * k, min(2 * k + 2, PREP)):
                                prepare(STRIPS * step.table + s, s, op)
                        if step.expert is not None:
                            q = STRIPS * step.expert + s
                            if k == 2 or k == 3 or k == 5:
                                mask_pixels(COLS * q + j, (k + 1) // 2)
                            if k == 8:
                                if not (last and j == COLS - 1):
                                    route(COLS * q + j + 1)
                                finish_output(q, j)
                        if last and step.refill is not None:
                            if TAPS + 2 <= l < TAPS + 2 + 20:
                                for n in range(2 * (l - TAPS - 2), 2 * (l - TAPS - 2) + 2):
                                    x_stat(step.refill, n)
                            if l == TAPS * (COLS - 1) + 3:
                                dve.wait_ge(x_stats, HALVES * STAT_PIECES * (step.refill + 1))
                                gn_before(chain_of[i, "x"], stat_x)
                            if l == TAPS * (COLS - 1) + 5:
                                gn_middle(chain_of[i, "x"])
                            if l == TAPS * (COLS - 1) + 7:
                                gn_after(chain_of[i, "x"], scale_x, shift_x, True)
                        if step.sample is not None and k == 0 and j:
                            finish_patch(STRIPS * step.sample + s, s, j - 1)

            for i, step in enumerate(STEPS):
                if step.sample is not None:
                    for l in range(2):
                        blend(STRIPS * step.sample, l)
                if step.expert is not None:
                    route(COLS * STRIPS * step.expert)
                each_strip(dve, step, lambda s, first, last: strip_body(i, step, s, first, last))
                if step.only_refill:
                    dve.wait_ge(weights_in, 16 * 3)
                    by_expert = wexp[:, :, :].rearrange("p (e h) n -> p e (h n)", e=EXPERTS)
                    nc.vector.tensor_tensor(by_expert[:, 1:EXPERTS, :], by_expert[:, 1:EXPERTS, :],
                                            by_expert[:, 0:1, :].to_broadcast([P, EXPERTS - 1, HALVES * CH]),
                                            ALU.subtract).then_inc(consts_made, 1)
                    dve.wait_ge(consts_made, 2)
                    nc.vector.tensor_tensor(wexp[:, 0:HALVES, :].rearrange("p h n -> p (h n)"),
                                            wexp[:, 0:HALVES, :].rearrange("p h n -> p (h n)"),
                                            xm[:, 0, :, :].rearrange("p h n -> p (h n)"), ALU.add).then_inc(consts_made, 1)
                if step.sample is not None:
                    finish_patch(STRIPS * step.sample + STRIPS - 1, STRIPS - 1, COLS - 1)
                    dve.wait_ge(x1_stats, HALVES * COLS * STRIPS * (step.sample + 1))
                    gn_before(chain_of[i, "x1"], stat_x1)
                    gn_middle(chain_of[i, "x1"])
                    gn_after(chain_of[i, "x1"], scale_x1, shift_x1, False)


def kernel(x, L0_conv_w_off, L0_conv_w_deform, L1_conv_Wr, L1_conv_We, L1_conv_Ws):
    import numpy as np
    import concourse.bacc as bacc
    from concourse.bass_utils import run_bass_kernel_spmd

    p = np.arange(P)
    tile = np.arange(STRIP_TILES)[None, :, None]
    tap = np.arange(TAPS)[None, None, :]
    py = (tile % TILES) * 8 + p[:, None, None] // PATCH + tap // 3 - 1
    px = (tile // TILES) * PATCH + p[:, None, None] % PATCH + tap % 3 - 1
    position = np.stack([np.broadcast_to(a, (P, STRIP_TILES, TAPS)) for a in (py, px)], 1)
    position = position.reshape(P, 2, STRIP_TILES * TAPS).astype(np.float32)
    strip_row = np.broadcast_to(np.arange(STRIPS) * PATCH, (P, STRIPS)).astype(np.float32)
    ident = np.eye(P, dtype=np.float32)
    group_mean = np.kron(np.eye(P // GROUP), np.full((GROUP, GROUP), 1 / GROUP)).astype(np.float32)
    sum_parts = np.tile(np.eye(P // QUADS, OFFS), (QUADS, 1)).astype(np.float32)
    first_wins = np.broadcast_to(EXPERTS - np.arange(EXPERTS), (P, TILES, EXPERTS)).astype(np.float32)

    arrays = {
        "x_in": np.asarray(x).reshape(IMAGES, HALVES, P, SIDE * SIDE),
        "w_offset": np.asarray(L0_conv_w_off).reshape(OFFS, HALVES, P, TAPS).transpose(2, 3, 1, 0)
        .reshape(P, TAPS * HALVES, OFFS),
        "w_deform": np.asarray(L0_conv_w_deform).reshape(CH, HALVES, P, TAPS).transpose(2, 3, 1, 0)
        .reshape(P, TAPS * HALVES, CH),
        "w_router": np.asarray(L1_conv_Wr).reshape(HALVES, P, EXPERTS).transpose(1, 0, 2),
        "w_expert": np.asarray(L1_conv_We).reshape(EXPERTS, HALVES, P, CH).transpose(2, 0, 1, 3)
        .reshape(P, EXPERTS * HALVES, CH),
        "w_shared": np.asarray(L1_conv_Ws).reshape(HALVES, P, CH).transpose(1, 0, 2),
        "ident": ident, "group_mean": group_mean, "position": position,
        "strip_row": strip_row, "first_wins": first_wins, "sum_parts": sum_parts,
    }
    arrays = {name: np.ascontiguousarray(a) for name, a in arrays.items()}
    nc = bacc.Bacc("TRN2", target_bir_lowering=False, num_devices=1, dynamic_dma_scratch_size=4096)
    args = [nc.dram_tensor(f"{name}_dram", a.shape, mybir.dt.from_np(a.dtype), kind="ExternalInput").ap()
            for name, a in arrays.items()]
    out = nc.dram_tensor("out_dram", (IMAGES, HALVES, P, SIDE * SIDE), F32, kind="ExternalOutput").ap()
    build(nc, *args, out)
    r = run_bass_kernel_spmd(nc, [{f"{name}_dram": a for name, a in arrays.items()}], core_ids=[0])
    return r.results[0]["out_dram"].reshape(IMAGES, CH, SIDE, SIDE)
```

```python
from contextlib import ExitStack

import concourse.bass as bass
from concourse import mybir

F32 = mybir.dt.float32
BF16 = mybir.dt.bfloat16
I32 = mybir.dt.int32
U32 = mybir.dt.uint32
ALU = mybir.AluOpType
ACT = mybir.ActivationFunctionType
AX = mybir.AxisListType

P = 128
IMAGES, CH, SIDE = 4, 256, 80
HALVES = CH // P
TAPS = 9
PATCH = 16
STRIPS = SIDE // PATCH
COLS = SIDE // PATCH
TILES = 2
PIX = PATCH * PATCH
STRIP_PIX = PATCH * SIDE
STRIP_TILES = COLS * TILES
EXPERTS = 4
OFFS = 2 * TAPS
GROUP = 8

RIM = 2
WIDE = SIDE + 2 * RIM
ENTRIES = (SIDE + 2 * RIM - 1) * WIDE
TROW = 112
TURNS = WIDE * PATCH // TROW
CHUNK = 2
CHUNKS = TURNS // CHUNK

PAIRS = COLS * TAPS
UNITS = PAIRS * TILES
RING = 10
STRIP_RING = STRIPS + 1
QUADS = 4
PART_ROUNDS = -(-TAPS * HALVES // QUADS)
CHUNK_FROM, CHUNK_SLOTS = 9, 5
PART_SLOTS = PART_ROUNDS + 2
STAT_PIX = 320
STAT_PIECES = SIDE * SIDE // STAT_PIX
STAT_FROM, STAT_TO = 8, 39
LOAD_SLOTS = 2
PREP = 10
STAGE = 3 * HALVES
EPS = 1e-5
SETS = 3
START = 1


class Step:

    def __init__(self, b):
        self.sample = b if 0 <= b < IMAGES else None
        self.table = b + 1 if 0 <= b + 1 < IMAGES else None
        self.refill = b + 2 if b + 2 < IMAGES else None
        self.expert = b - 1 if 0 <= b - 1 < IMAGES else None
        self.last_sample = b == IMAGES - 1
        self.only_refill = b == -2
        self.only_table = b == -1
        self.only_expert = b == IMAGES


STEPS = [Step(b) for b in range(-2, IMAGES + 1)]


def each_strip(eng, step, body):
    if step.only_table:
        for s in range(STRIPS - 1):
            body(s, s == 0, False)
    elif not step.only_refill:
        body(0, True, False)
        with eng.Fori(1, STRIPS - 1) as s:
            body(s, False, False)
    body(STRIPS - 1, False, True)


def chunk_beside(l):
    c, rest = divmod(l - CHUNK_FROM, CHUNK_SLOTS)
    return c if rest == 0 and 0 <= c < CHUNKS else None


def gn_chains():
    at, n = {}, 0
    for i, step in enumerate(STEPS):
        if step.refill is not None:
            at[i, "x"] = n
            n += 1
        if step.sample is not None:
            at[i, "x1"] = n
            n += 1
    return at


GN_A, GN_B, GN_C = 4, 4, 3
GN_OPS = GN_A + GN_B + GN_C


def build(nc, x, w_offset, w_deform, w_router, w_expert, w_shared, ident, group_mean, position,
          strip_row, first_wins, sum_parts, out):
    chain_of = gn_chains()
    tables = [nc.dram_tensor(f"table{b}", [ENTRIES, 2 * CH], F32, kind="Internal") for b in range(IMAGES)]

    with ExitStack() as ctx:
        def sb(name, shape, dt=F32):
            return ctx.enter_context(nc.sbuf_tensor(name, shape, dt))

        def pb(name, shape):
            return ctx.enter_context(nc.psum_tensor(name, shape, F32))

        def sem(name):
            return ctx.enter_context(nc.semaphore(name))

        idn = sb("idn", [P, P])
        idn_bf = sb("idn_bf", [P, P], BF16)
        gmean = sb("gmean", [P, P])
        posc = sb("posc", [P, 2, STRIP_TILES * TAPS])
        srow = sb("srow", [P, STRIPS])
        order = sb("order", [P, TILES, EXPERTS])
        woff = sb("woff", [P, TAPS * HALVES, P // QUADS])
        pick = sb("pick", [P, OFFS])
        wdef = sb("wdef", [P, TAPS * HALVES, CH])
        wrt = sb("wrt", [P, HALVES, EXPERTS])
        wexp = sb("wexp", [P, EXPERTS * HALVES, CH])
        xin = sb("xin", [P, HALVES, SIDE + 2, SIDE])
        strip = sb("strip", [P, HALVES, PATCH + 2, WIDE])
        turned = sb("turned", [TROW, 2, CHUNK, CH])
        stat_x = sb("stat_x", [P, HALVES, STAT_PIECES, 6])
        part = sb("part", [P, PIX])
        pyx = sb("pyx", [P, 2, STRIP_TILES * TAPS])
        whole = sb("whole", [P, 2, STRIP_TILES * TAPS], I32)
        floor = whole[:, :, :].bitcast(F32)
        entry_img = sb("entry_img", [P, STRIPS * STRIP_TILES, TAPS], U32)
        frac_img = sb("frac_img", [P, 2, STRIPS * STRIP_TILES * TAPS])
        entry = [sb(f"entry{j}", [P, TILES, TAPS], U32) for j in range(COLS)]
        near_far = sb("near_far", [P, 2, 2, TILES * TAPS])
        weight = [sb(f"weight{j}", [P, TILES, TAPS, 4]) for j in range(COLS)]
        corners = sb("corners", [P, RING, 4 * CH])
        val = sb("val", [P, 2, HALVES, PIX])
        x1 = sb("x1", [P, STRIP_RING, HALVES, PATCH, SIDE])
        stat_x1 = sb("stat_x1", [P, HALVES, STRIPS * COLS, 6])
        xn = sb("xn", [P, HALVES, PIX])
        xm = sb("xm", [P, 2, HALVES, PIX])
        top = sb("top", [P, TILES])
        score = sb("score", [P, TILES, EXPERTS])
        mask = sb("mask", [P, TILES, EXPERTS], BF16)
        mv = sb("mv", [P, HALVES, 2])
        small = sb("small", [P, 3, HALVES])
        sq = small[:, 0, :]
        gmv = sb("gmv", [P, HALVES, 2])
        gsq = sq
        gvar = small[:, 1, :]
        root = gvar
        affine = sb("affine", [P, 4, HALVES])
        scale_x, shift_x, scale_x1, shift_x1 = (affine[:, n, :] for n in range(4))
        shift_below = sb("shift_below", [P, STRIPS, HALVES])
        zero = small[:, 2, 0:1]

        p_turn = [pb(f"p_turn{i}", [P, HALVES * PIX]) for i in range(2)]
        p_acc = [pb(f"p_acc{i}", [P, HALVES * PIX]) for i in range(2)]
        p_part = pb("p_part", [P, PIX + STRIP_TILES * OFFS])
        p_offs = p_part[:, PIX:PIX + STRIP_TILES * OFFS]
        p_table_bank = pb("p_table", [P, CHUNK * CH])
        p_table = p_table_bank[:, :].rearrange("p (i c) -> p i c", i=CHUNK)
        p_route = pb("p_route", [P, 512])
        p_logits = p_route[:, 0:TILES * EXPERTS]
        p_moe = pb("p_moe", [P, HALVES * PIX])

        consts_in = sem("consts_in")
        weights_in = sem("weights_in")
        zeroed = sem("zeroed")
        consts_made = sem("consts_made")
        rim_out = sem("rim_out")
        x_in = [sem(f"x_in{i}") for i in range(STRIPS)]
        x_stats = sem("x_stats")
        gn_dve = sem("gn_dve")
        gn_sums = sem("gn_sums")
        gn_root = sem("gn_root")
        staged = sem("staged")
        part_done = sem("part_done")
        part_copied = sem("part_copied")
        offs_done = sem("offs_done")
        table_turned = sem("table_turned")
        table_copied = sem("table_copied")
        table_out = [sem(f"table_out{i}") for i in range(2)]
        prepped = sem("prepped")
        picked = sem("picked")
        gathered = [sem(f"gathered{i}") for i in range(RING)]
        unit_free = sem("unit_free")
        unit_taken = sem("unit_taken")
        scaled = sem("scaled")
        blended = sem("blended")
        val_ready = sem("val_ready")
        conv_done = sem("conv_done")
        resid_in = sem("resid_in")
        x1_done = sem("x1_done")
        x1_stats = sem("x1_stats")
        xn_ready = sem("xn_ready")
        logits_done = sem("logits_done")
        routed = sem("routed")
        mask_done = sem("mask_done")
        xm_ready = sem("xm_ready")
        moe_done = sem("moe_done")
        out_ready = sem("out_ready")
        out_stored = sem("out_stored")

        PICKED = 6
        ROUTE = 5
        ZEROED = 7
        CONSTS = 8

        started = {
            "sync": [(table_out[0], 16), (table_out[1], 16), (out_stored, 16)],
            "scalar": [(val_ready, 1), (part_copied, 1), (table_copied, 1)],
            "tensor": [(conv_done, 1), (mask_done, 1), (moe_done, 1)],
            "vector": [(x1_done, 1), (xm_ready, 1), (out_ready, 1), (prepped, 1)],
        }

        def start(eng, name):
            for counter, unit in started[name]:
                eng.sem_inc(counter, START * unit)

        def reuse(n, l):
            return n if isinstance(l, int) and l == 0 else n - 1

        spare = corners[:, :, :].rearrange("p u (b h n) -> p (u b) h n", b=2, h=HALVES)

        def expert_buffers(final, j):
            if not final:
                return xn, [xm[:, (e - 1) % 2, :, :] for e in range(1, EXPERTS)], p_route[:, P:512], p_moe
            n = j % SETS
            return (spare[:, EXPERTS * n, :, :], [spare[:, EXPERTS * n + e, :, :] for e in range(1, EXPERTS)],
                    [p_turn[0], p_turn[1], p_table_bank][n][:, P:512], [p_moe, p_acc[0], p_acc[1]][n])

        strip_odd = x1[:, STRIP_RING - 2:STRIP_RING, :, :, :].rearrange("p q h r c -> p (q h r c)")[
            :, 0:HALVES * (PATCH + 2) * WIDE].rearrange("p (h r c) -> p h r c", h=HALVES, c=WIDE)
        strip_bufs = [strip, strip_odd]
        part_bufs = [part[:, :], val[:, 0, 0, :]]
        table_banks = [p_table, p_moe[:, :].rearrange("p (i c) -> p i c", i=CHUNK)]
        part_banks = [p_part, p_acc[0]]
        offs_banks = [p_turn[n][:, 0:STRIP_TILES * OFFS] for n in range(2)]

        def by_expert_mask(bank):
            return bank.bitcast(BF16).rearrange("p (e n) -> p e n", e=EXPERTS - 1)

        block = ctx.enter_context(nc.Block())

        @block.sync
        def _(sp):
            start(sp, "sync")

            def load_x(image, i):
                sp.dma_start(xin[:, :, 1 + PATCH * i:1 + PATCH * (i + 1), :].rearrange("p h r c -> p h (r c)"),
                             x[image, :, :, STRIP_PIX * i:STRIP_PIX * (i + 1)].rearrange("h p n -> p h n")
                             ).then_inc(x_in[i], 16)

            load_x(0, 0)
            sp.dma_start(idn[:, :], ident).then_inc(consts_in, 16)
            sp.dma_start(gmean[:, :], group_mean).then_inc(consts_in, 16)
            sp.dma_start(posc[:, :, :], position).then_inc(consts_in, 16)
            sp.dma_start(srow[:, :], strip_row).then_inc(consts_in, 16)
            sp.dma_start(order[:, :, :], first_wins).then_inc(consts_in, 16)
            sp.dma_start(wrt[:, :, :], w_router).then_inc(consts_in, 16)
            sp.dma_start(pick[:, :], sum_parts).then_inc(consts_in, 16)
            for i in range(1, STRIPS):
                load_x(0, i)
            sp.wait_ge(zeroed, ZEROED)
            sp.dma_start(woff[:, :, 0:OFFS], w_offset).then_inc(consts_in, 16)

            def rims():
                zeros = strip[0:WIDE, 0, :, :].rearrange("p r c -> p (r c)")
                for t in tables:
                    last = ENTRIES - WIDE
                    sp.dma_start(t[0:WIDE, :], zeros[:, 0:2 * CH]).then_inc(rim_out, 16)
                    sp.dma_start(t[WIDE:2 * WIDE, 0:CH], zeros[:, 0:CH]).then_inc(rim_out, 16)
                    sp.dma_start(t[last - WIDE:last, CH:2 * CH], zeros[:, 0:CH]).then_inc(rim_out, 16)
                    sp.dma_start(t[last:ENTRIES, :], zeros[:, 0:2 * CH]).then_inc(rim_out, 16)

            def strip_body(step, s, last):
                if step.sample is not None:
                    q = STRIPS * step.sample + s
                    if step.expert is not None:
                        sp.wait_ge(out_stored, 16 * START + (q - STRIPS) * 16)
                    sp.dma_start(x1[:, bass.ds(q % STRIP_RING, 1), :, :, :].rearrange("p o h r c -> p (o h) (r c)"),
                                 x[step.sample, :, :, bass.ds(STRIP_PIX * s, STRIP_PIX)].rearrange("h p n -> p h n")
                                 ).then_inc(resid_in, 16)
                if step.only_table:
                    if s > 0:
                        sp.wait_ge(staged, STAGE * (s + 1))
                        for i in range(s - 1, STRIPS if last else s):
                            load_x(step.refill, i)
                elif last and step.sample is not None and step.refill is not None:
                    sp.wait_ge(staged, STAGE * STRIPS * (step.table + 1))
                    for i in range(STRIPS):
                        sp.wait_ge(conv_done, START + PAIRS * (STRIPS * step.sample + s) + LOAD_SLOTS * i + 1)
                        load_x(step.refill, i)
                if step.table is not None:
                    t = tables[step.table]
                    for c in range(CHUNKS):
                        sp.wait_ge(table_copied, START + CHUNKS * (STRIPS * step.table + s) + c + 1)
                        f = (PATCH * s + RIM) * WIDE + TROW * CHUNK * c
                        src = turned[:, c % 2, :, :]
                        sp.dma_start(t[bass.ds(f, TROW * CHUNK), 0:CH].rearrange("(i p) c -> p i c", p=TROW),
                                     src).then_inc(table_out[c % 2], 16)
                        sp.dma_start(t[bass.ds(f - WIDE, TROW * CHUNK), CH:2 * CH].rearrange("(i p) c -> p i c", p=TROW),
                                     src).then_inc(table_out[c % 2], 16)
                if step.expert is not None:
                    q = STRIPS * step.expert + s
                    sp.wait_ge(out_ready, START + COLS * (q + 1))
                    sp.dma_start(out[step.expert, :, :, bass.ds(STRIP_PIX * s, STRIP_PIX)].rearrange("h p n -> p h n"),
                                 x1[:, bass.ds(q % STRIP_RING, 1), :, :, :].rearrange("p o h r c -> p (o h) (r c)")
                                 ).then_inc(out_stored, 16)

            for i, step in enumerate(STEPS):
                each_strip(sp, step, lambda s, first, last: strip_body(step, s, last))
                if step.only_refill:
                    rims()
                    sp.dma_start(wdef[:, :, :], w_deform).then_inc(weights_in, 16)
                    sp.dma_start(wexp[:, :, :], w_expert).then_inc(weights_in, 16)
                    sp.dma_start(xm[:, 0, :, :], w_shared).then_inc(weights_in, 16)
            sp.wait_ge(out_stored, 16 * START + 16 * STRIPS * IMAGES)

        @block.gpsimd
        def _(pool):
            nc.gpsimd.memset(strip[:, :, :, :], 0.0).then_inc(zeroed, 1)
            nc.gpsimd.memset(xin[:, :, 0:1, :], 0.0).then_inc(zeroed, 1)
            nc.gpsimd.memset(xin[:, :, SIDE + 1:SIDE + 2, :], 0.0).then_inc(zeroed, 1)
            nc.gpsimd.memset(shift_below[:, :, :], 0.0).then_inc(zeroed, 1)
            nc.gpsimd.memset(zero, 0.0).then_inc(zeroed, 1)
            nc.gpsimd.memset(woff[:, :, :], 0.0).then_inc(zeroed, 1)
            nc.gpsimd.memset(strip_odd, 0.0).then_inc(zeroed, 1)
            nc.gpsimd.memset(corners[:, 0, 0:1], 0.0).then_inc(unit_free, RING)
            pool.wait_ge(unit_free, RING)

            def strip_body(step, s, last):
                q = STRIPS * step.sample + s
                for j in range(COLS):
                    g = COLS * q + j
                    tile = STRIP_TILES * s + TILES * j
                    nc.gpsimd.tensor_copy(entry[j][:, :, :], entry_img[:, bass.ds(tile, TILES), :]).then_inc(picked, 1)
                    frac = frac_img[:, :, bass.ds(tile * TAPS, TILES * TAPS)]
                    nc.gpsimd.tensor_copy(near_far[:, :, 1, :], frac).then_inc(picked, 1)
                    pool.wait_ge(picked, PICKED * g + 2).then_inc(picked, 1)
                    nc.gpsimd.tensor_scalar(near_far[:, :, 0, :], near_far[:, :, 1, :], -1.0, 1.0,
                                            ALU.mult, ALU.add).then_inc(picked, 1)
                    pool.wait_ge(picked, PICKED * g + 4)
                    for c in range(2):
                        nc.gpsimd.tensor_tensor(
                            weight[j][:, :, :, 2 * c:2 * c + 2].rearrange("p t k c -> p c (t k)"), near_far[:, 0, :, :],
                            near_far[:, 1, c:c + 1, :].to_broadcast([P, 2, TILES * TAPS]), ALU.mult).then_inc(picked, 1)
                    pool.wait_ge(picked, PICKED * (g + 1))
                    for v in range(UNITS // COLS):
                        k, t = divmod(v, TILES)
                        local = UNITS // COLS * j + v
                        pool.wait_ge(unit_free, UNITS * q + local + 1).then_inc(unit_taken, 1)
                        nc.gpsimd.indirect_dma_start(
                            corners[:, local % RING, :], None, tables[step.sample][:, :],
                            bass.IndirectOffsetOnAxis(ap=entry[j][:, t, k:k + 1], axis=0),
                        ).then_inc(gathered[local % RING], 16)

            for step in STEPS:
                if step.sample is not None:
                    pool.wait_ge(prepped, START + PREP * STRIPS * (step.sample + 1))
                    pool.wait_ge(rim_out, 16 * 4 * IMAGES)
                    for half in range(2):
                        pool.wait_ge(table_out[half], 16 * START + 16 * CHUNKS * STRIPS * (step.sample + 1))
                    each_strip(pool, step, lambda s, first, last: strip_body(step, s, last))

        @block.scalar
        def _(act):
            start(act, "scalar")
            act.wait_ge(zeroed, ZEROED)

            def scale_corner(q, l):
                j, k = divmod(l % PAIRS, TAPS)
                for t in range(TILES):
                    local = TILES * (l % PAIRS) + t
                    act.wait_ge(gathered[local % RING], 16 * (UNITS // RING * (q + l // PAIRS) + local // RING + 1))
                    c = corners[:, local % RING, 0:CH]
                    nc.scalar.activation(c, c, ACT.Identity, bias=zero,
                                         scale=weight[j][:, t, k, 0:1]).then_inc(scaled, 1)

            def copy_val(q, l):
                n = PAIRS * q + l
                act.wait_ge(unit_free, RING + TILES * (n + 1))
                act.wait_ge(conv_done, START + reuse(n, l % PAIRS))
                b = l % PAIRS % 2
                nc.scalar.activation(val[:, b, :, :].rearrange("p h n -> p (h n)"), p_turn[b][:, :],
                                     ACT.Copy).then_inc(val_ready, 1)

            def stage(s, piece, edge_row, strip=strip):
                h, piece = divmod(piece, 3)
                sc = scale_x[:, h:h + 1]
                cols = slice(RIM, RIM + SIDE)
                if piece == 0:
                    nc.scalar.activation(strip[:, h, 1:1 + PATCH, cols], xin[:, h, bass.ds(PATCH * s + 1, PATCH), :],
                                         ACT.Identity, bias=shift_x[:, h:h + 1], scale=sc).then_inc(staged, 1)
                elif piece == 1:
                    bias = zero if edge_row else shift_x[:, h:h + 1]
                    nc.scalar.activation(strip[:, h, 0:1, cols], xin[:, h, bass.ds(PATCH * s, 1), :],
                                         ACT.Identity, bias=bias, scale=sc).then_inc(staged, 1)
                else:
                    nc.scalar.activation(strip[:, h, 1 + PATCH:2 + PATCH, cols],
                                         xin[:, h, bass.ds(PATCH * (s + 1) + 1, 1), :], ACT.Identity,
                                         bias=shift_below[:, bass.ds(s, 1), h], scale=sc).then_inc(staged, 1)

            def normalize_patch(q, j, final):
                g = COLS * q + j
                q, j = q + j // COLS, j % COLS
                pixels = expert_buffers(final, j)[0]
                if final:
                    act.wait_ge(xm_ready, START + (EXPERTS - 1) * (g - 1))
                    act.wait_ge(moe_done, START + EXPERTS * (g - 2) + 1)
                else:
                    act.wait_ge(xm_ready, START + (EXPERTS - 1) * g)
                    if not (isinstance(g, int) and g == 0):
                        act.wait_ge(moe_done, START + EXPERTS * (g - 1) + 1)
                for h in range(HALVES):
                    nc.scalar.activation(
                        pixels[:, h, :].rearrange("p (r c) -> p r c", c=PATCH),
                        x1[:, bass.ds(q % STRIP_RING, 1), h, :, PATCH * j:PATCH * (j + 1)]
                        .rearrange("p o r c -> p (o r) c"),
                        ACT.Identity, bias=shift_x1[:, h:h + 1], scale=scale_x1[:, h:h + 1]
                    ).then_inc(xn_ready, 1)

            def copy_part(g, bank, to):
                act.wait_ge(part_done, g + 1)
                nc.scalar.activation(to, bank[:, 0:PIX], ACT.Copy).then_inc(part_copied, 1)

            def copy_chunk(q, c, bank):
                act.wait_ge(table_turned, CHUNKS * q + c + 1)
                act.wait_ge(table_out[c % 2], 16 * START + 16 * 2 * (CHUNKS // 2 * q + c // 2))
                nc.scalar.activation(turned[:, c % 2, :, :], bank[0:TROW, :, :], ACT.Copy).then_inc(table_copied, 1)

            def first_table_body(i, step, s, last):
                for j in range(COLS):
                    g = COLS * s + j
                    copy_part(g, part_banks[g % 2], part_bufs[g % 2])
                    copy_chunk(s, j, table_banks[j % 2])
                    if not last:
                        if j == 0:
                            act.wait_ge(part_done, COLS * s)
                            act.wait_ge(table_turned, CHUNKS * s)
                        for piece in [(0,), (1, 2), (3,), (4, 5), ()][j]:
                            stage(s + 1, piece, False, strip_bufs[(s + 1) % 2])
                copy_chunk(s, CHUNKS - 1, table_banks[(CHUNKS - 1) % 2])
                if last:
                    gn_take_root(chain_of[i, "x"])
                    act.wait_ge(gn_dve, GN_OPS * (chain_of[i, "x"] + 1))
                    act.wait_ge(offs_done, STRIPS * (step.table + 1))
                    for piece in range(STAGE):
                        stage(0, piece, True)

            def gn_take_root(chain):
                act.wait_ge(gn_dve, GN_OPS * chain + GN_A + GN_B)
                nc.scalar.activation(root, gvar, ACT.Sqrt).then_inc(gn_root, 1)

            def final_body(step, s, last):
                for j in range(COLS - 2 if last else COLS):
                    normalize_patch(STRIPS * step.expert + s, j + 2, True)

            def strip_body(i, step, s, last):
                if step.only_expert:
                    final_body(step, s, last)
                    return
                if step.only_table:
                    first_table_body(i, step, s, last)
                    return
                for j in range(COLS):
                    for k in range(TAPS):
                        l = TAPS * j + k
                        if step.sample is not None:
                            q = STRIPS * step.sample + s
                            if not (last and step.last_sample and l + 1 >= PAIRS):
                                copy_val(q, l + 1)
                        if step.table is not None and chunk_beside(l - 1) is not None:
                            copy_chunk(STRIPS * step.table + s, chunk_beside(l - 1), p_table)
                        if step.table is not None and l < PART_SLOTS * COLS and l % PART_SLOTS == PART_ROUNDS:
                            copy_part(COLS * (STRIPS * step.table + s) + l // PART_SLOTS, p_part, part[:, :])
                        if step.sample is not None and not (last and step.last_sample and l + 3 >= PAIRS):
                            scale_corner(STRIPS * step.sample + s, l + 3)
                        if step.expert is not None and k == 7 and not (last and j == COLS - 1):
                            normalize_patch(STRIPS * step.expert + s, j + 1, False)
                        if j == COLS - 1:
                            if last and step.refill is not None:
                                if k == 5:
                                    gn_take_root(chain_of[i, "x"])
                                if k == 8:
                                    act.wait_ge(gn_dve, GN_OPS * (chain_of[i, "x"] + 1))
                                    if step.table is not None:
                                        act.wait_ge(offs_done, STRIPS * (step.table + 1))
                                    else:
                                        act.wait_ge(rim_out, 16 * 4 * IMAGES)
                                    for piece in range(STAGE):
                                        stage(0, piece, True)
                            elif not last and step.table is not None and 2 <= k < 2 + STAGE:
                                act.wait_ge(offs_done, STRIPS * step.table + s + 1)
                                stage(s + 1, k - 2, False)

            for i, step in enumerate(STEPS):
                if step.sample == 0:
                    for l in range(3):
                        scale_corner(0, l)
                    copy_val(0, 0)
                if step.expert is not None:
                    act.wait_ge(gn_dve, GN_OPS * (chain_of[i - 1, "x1"] + 1))
                    for j in range(2 if step.only_expert else 1):
                        normalize_patch(STRIPS * step.expert, j, step.only_expert)
                each_strip(act, step, lambda s, first, last: strip_body(i, step, s, last))
                if step.sample is not None:
                    gn_take_root(chain_of[i, "x1"])

        @block.tensor
        def _(pe):
            start(pe, "tensor")
            pe.wait_ge(consts_in, 16 * CONSTS)

            def turn_pair(q, l):
                n = PAIRS * q + l
                l = l % PAIRS
                pe.wait_ge(val_ready, START + reuse(n, l))
                for t in range(TILES):
                    pe.wait_ge(blended, 6 * n + 5 + t)
                    unit = (TILES * l + t) % RING
                    for h in range(HALVES):
                        mm = nc.tensor.transpose(p_turn[l % 2][:, PIX * h + P * t:PIX * h + P * (t + 1)],
                                                 corners[:, unit, P * h:P * (h + 1)], idn[:, :])
                    mm.then_inc(unit_free, 1)

            def conv_pair(q, l):
                j, k = divmod(l, TAPS)
                n = PAIRS * q + l
                pe.wait_ge(val_ready, START + n + 1)
                if k == 0:
                    pe.wait_ge(x1_done, START + COLS * q + (j if j == 0 else j - 1))
                for m in range(HALVES):
                    for h in range(HALVES):
                        mm = nc.tensor.matmul(p_acc[j % 2][:, PIX * m:PIX * (m + 1)],
                                              wdef[:, HALVES * k + h, P * m:P * (m + 1)], val[:, l % 2, h, :],
                                              start=(k == 0 and h == 0 and m == 0), stop=(k == TAPS - 1),
                                              skip_group_check=True)
                mm.then_inc(conv_done, 1)

            def part_round(j, i, strip, bank):
                for kh in range(QUADS * i, min(QUADS * (i + 1), TAPS * HALVES)):
                    k, h = divmod(kh, HALVES)
                    c = P // QUADS * (kh % QUADS)
                    row, col = k // 3, PATCH * j + k % 3 + RIM - 1
                    mm = nc.tensor.matmul(bank[c:c + P // QUADS, 0:PIX], woff[:, kh, :],
                                          strip[:, h, row:row + PATCH, col:col + PATCH],
                                          start=(i == 0), stop=(kh + QUADS >= TAPS * HALVES))
                if i == PART_ROUNDS - 1:
                    mm.then_inc(part_done, 1)

            def add_parts(g, j, parts, offs):
                pe.wait_ge(part_copied, START + g + 1)
                for t in range(TILES):
                    at = OFFS * (TILES * j + t)
                    mm = nc.tensor.matmul(offs[:, at:at + OFFS], parts[:, P * t:P * (t + 1)], pick[:, :],
                                          start=True, stop=True)
                if j == COLS - 1:
                    mm.then_inc(offs_done, 1)

            def offset_part(q, l):
                j, i = divmod(l, PART_SLOTS)
                g = COLS * q + j
                if i == 0:
                    pe.wait_ge(part_copied, START + g)
                if i < PART_ROUNDS:
                    part_round(j, i, strip, p_part)
                elif i == PART_ROUNDS + 1:
                    add_parts(g, j, part, p_offs)

            def turn_chunk(c, strip, bank):
                for i in range(CHUNK):
                    for h in range(HALVES):
                        rows = strip[:, h, :, :].rearrange("p r c -> p (r c)")
                        at = WIDE + TROW * (CHUNK * c + i)
                        mm = nc.tensor.transpose(bank[0:TROW, i, P * h:P * (h + 1)],
                                                 rows[:, at:at + TROW], idn[:, :])
                mm.then_inc(table_turned, 1)

            def table_turn(q, c):
                pe.wait_ge(table_copied, START + CHUNKS * q + c)
                turn_chunk(c, strip, p_table)

            def first_table_body(i, step, s, last):
                pe.wait_ge(staged, STAGE * (s + 1))
                for j in range(COLS + 1):
                    g = COLS * s + j
                    if j < COLS:
                        if g >= 2:
                            pe.wait_ge(part_copied, START + g - 1)
                        for n in range(PART_ROUNDS):
                            part_round(j, n, strip_bufs[s % 2], part_banks[g % 2])
                    if j < CHUNKS:
                        if CHUNKS * s + j >= 2:
                            pe.wait_ge(table_copied, START + CHUNKS * s + j - 1)
                        turn_chunk(j, strip_bufs[s % 2], table_banks[j % 2])
                    if j > 0:
                        if j == 1 and s >= 2:
                            pe.wait_ge(prepped, START + PREP * (s - 1))
                        add_parts(g - 1, j - 1, part_bufs[(g - 1) % 2], offs_banks[s % 2])
                if last:
                    gn_group_sums(chain_of[i, "x"], CHUNKS * STRIPS * (step.table + 1))

            def gn_group_sums(chain, tables_done):
                pe.wait_ge(gn_dve, GN_OPS * chain + GN_A)
                pe.wait_ge(table_copied, START + tables_done)
                nc.tensor.matmul(p_table[:, 0, 0:2 * HALVES], gmean[:, :],
                                 mv[:, :, :].rearrange("p h v -> p (h v)"), start=True, stop=True
                                 ).then_inc(gn_sums, 1)

            def logits(g, j, final):
                pixels = expert_buffers(final, j % COLS)[0]
                pe.wait_ge(xn_ready, HALVES * (g + 1))
                for t in range(TILES):
                    for h in range(HALVES):
                        mm = nc.tensor.matmul(p_logits[:, EXPERTS * t:EXPERTS * (t + 1)], pixels[:, h, P * t:P * (t + 1)],
                                              wrt[:, h, :], start=(h == 0), stop=(h == HALVES - 1))
                mm.then_inc(logits_done, 1)

            def spread_masks(g, j, final):
                masks = by_expert_mask(expert_buffers(final, j % COLS)[2])
                pe.wait_ge(routed, ROUTE * (g + 1))
                for e in range(1, EXPERTS):
                    for t in range(TILES):
                        mm = nc.tensor.transpose(masks[:, e - 1, P * t:P * (t + 1)],
                                                 mask[:, t, e:e + 1].to_broadcast([P, P]), idn_bf[:, :])
                mm.then_inc(mask_done, 1)

            def expert_products(g, j, e, halves, final):
                every, own, _, bank = expert_buffers(final, j)
                if e == 0 and 0 in halves:
                    pe.wait_ge(xn_ready, HALVES * (g + 1))
                    pe.wait_ge(out_ready, START + (g - 1 if final else g))
                elif 0 in halves:
                    pe.wait_ge(xm_ready, START + (EXPERTS - 1) * g + e)
                for m in halves:
                    for h in range(HALVES):
                        pixels = own[e - 1][:, h, :] if e else every[:, h, :]
                        mm = nc.tensor.matmul(bank[:, PIX * m:PIX * (m + 1)],
                                              wexp[:, HALVES * e + h, P * m:P * (m + 1)], pixels,
                                              start=(e == 0 and h == 0 and m == 0), stop=(e == EXPERTS - 1),
                                              skip_group_check=True)
                if HALVES - 1 in halves:
                    mm.then_inc(moe_done, 1)

            def expert_part(q, j, k, last):
                g = COLS * q + j
                if k > 0:
                    expert_products(g, j, (k - 1) // HALVES, [(k - 1) % HALVES], False)
                if k == 1:
                    spread_masks(g, j, False)
                if k == TAPS - 1 and not (last and j == COLS - 1):
                    logits(g + 1, j + 1, False)

            def final_body(step, s, last):
                for j in range(COLS):
                    g = COLS * (STRIPS * step.expert + s) + j
                    ahead = not (last and j == COLS - 1)
                    if ahead:
                        logits(g + 1, j + 1, True)
                    expert_products(g, j, 1, range(HALVES), True)
                    if ahead:
                        spread_masks(g + 1, j + 1, True)
                    expert_products(g, j, 2, range(HALVES), True)
                    expert_products(g, j, 3, range(HALVES), True)
                    if ahead:
                        expert_products(g + 1, (j + 1) % COLS, 0, range(HALVES), True)

            def strip_body(i, step, s, last):
                if step.only_expert:
                    final_body(step, s, last)
                    return
                if step.only_table:
                    first_table_body(i, step, s, last)
                    return
                if step.table is not None:
                    q = STRIPS * step.table + s
                    pe.wait_ge(staged, STAGE * (q + 1))
                    pe.wait_ge(prepped, START + PREP * q)
                for j in range(COLS):
                    for k in range(TAPS):
                        l = TAPS * j + k
                        if step.sample is not None:
                            q = STRIPS * step.sample + s
                            if not (last and step.last_sample and l + 1 >= PAIRS):
                                turn_pair(q, l + 1)
                            conv_pair(q, l)
                        if step.table is not None and j < COLS - 1:
                            q = STRIPS * step.table + s
                            if chunk_beside(l) is not None:
                                table_turn(q, chunk_beside(l))
                            if l < PART_SLOTS * COLS:
                                offset_part(q, l)
                        if step.expert is not None:
                            expert_part(STRIPS * step.expert + s, j, k, last)
                        if last and step.refill is not None and l == TAPS * (COLS - 1) + 4:
                            done = 0 if step.table is None else CHUNKS * STRIPS * (step.table + 1)
                            gn_group_sums(chain_of[i, "x"], done)

            for i, step in enumerate(STEPS):
                if step.sample == 0:
                    pe.wait_ge(weights_in, 16 * 3)
                    pe.wait_ge(consts_made, 3)
                    turn_pair(0, 0)
                if step.expert is not None:
                    logits(COLS * STRIPS * step.expert, 0, step.only_expert)
                if step.only_expert:
                    expert_products(COLS * STRIPS * step.expert, 0, 0, range(HALVES), True)
                    spread_masks(COLS * STRIPS * step.expert, 0, True)
                each_strip(pe, step, lambda s, first, last: strip_body(i, step, s, last))
                if step.sample is not None:
                    tables_done = CHUNKS * STRIPS * min(step.sample + 2, IMAGES)
                    gn_group_sums(chain_of[i, "x1"], tables_done)

        @block.vector
        def _(dve):
            start(dve, "vector")

            def blend(q, l):
                n = PAIRS * q + l
                l = l % PAIRS
                j, k = divmod(l, TAPS)
                for c in range(1, 4):
                    for t in range(TILES):
                        unit = (TILES * l + t) % RING
                        if c == 1:
                            dve.wait_ge(scaled, TILES * n + t + 1)
                        else:
                            dve.wait_ge(blended, 6 * n + 2 * (c - 2) + t + 1)
                        acc = corners[:, unit, 0:CH]
                        nc.vector.scalar_tensor_tensor(
                            out=acc, in0=corners[:, unit, CH * c:CH * (c + 1)], scalar=weight[j][:, t, k, c:c + 1],
                            in1=acc, op0=ALU.mult, op1=ALU.add).then_inc(blended, 1)

            def finish_patch(q, s, j):
                g = COLS * q + j
                dve.wait_ge(conv_done, START + TAPS * (g + 1))
                if j == 0:
                    dve.wait_ge(resid_in, 16 * (q + 1))
                at = x1[:, bass.ds(q % STRIP_RING, 1), :, :, PATCH * j:PATCH * (j + 1)].rearrange(
                    "p o h r c -> p (o h) r c")
                nc.vector.tensor_tensor(at, p_acc[j % 2][:, :].rearrange("p (h r c) -> p h r c", h=HALVES, c=PATCH),
                                        at, ALU.add).then_inc(x1_done, 1)
                dve.wait_ge(x1_done, START + g + 1)
                for h in range(HALVES):
                    nc.vector.bn_stats(stat_x1[:, h, bass.ds(COLS * s + j, 1), :],
                                       x1[:, bass.ds(q % STRIP_RING, 1), h, :, PATCH * j:PATCH * (j + 1)]
                                       .rearrange("p o r c -> p (o r) c")).then_inc(x1_stats, 1)

            def prepare(q, s, op, offs=p_offs):
                offs = offs.rearrange("p (n v) -> p v n", v=2)
                row = bass.ds(STRIP_TILES * s, STRIP_TILES)
                if op == 0:
                    dve.wait_ge(offs_done, q + 1)
                elif op != 1:
                    dve.wait_ge(prepped, START + PREP * q + op)
                if op == 0:
                    ins = nc.vector.scalar_tensor_tensor(out=pyx[:, 0, :], in0=posc[:, 0, :], scalar=srow[:, bass.ds(s, 1)],
                                                         in1=offs[:, 0, :], op0=ALU.add, op1=ALU.add)
                elif op == 1:
                    ins = nc.vector.tensor_tensor(pyx[:, 1, :], posc[:, 1, :], offs[:, 1, :], ALU.add)
                elif op == 2:
                    ins = nc.vector.tensor_scalar(pyx[:, :, :], pyx[:, :, :], float(-RIM), SIDE + 0.5, ALU.max, ALU.min)
                elif op == 3:
                    ins = nc.vector.tensor_copy(whole[:, :, :], pyx[:, :, :])
                elif op == 4:
                    ins = nc.vector.tensor_copy(floor, whole[:, :, :])
                elif op == 5:
                    ins = nc.vector.tensor_tensor(pyx[:, :, :], pyx[:, :, :], floor, ALU.subtract)
                elif op == 6:
                    ins = nc.vector.scalar_tensor_tensor(
                        out=frac_img[:, :, bass.ds(STRIP_TILES * TAPS * s, STRIP_TILES * TAPS)], in0=pyx[:, :, :],
                        scalar=0.0, in1=pyx[:, :, :], op0=ALU.is_lt, op1=ALU.add)
                elif op == 7:
                    ins = nc.vector.scalar_tensor_tensor(out=floor, in0=pyx[:, :, :], scalar=0.0, in1=floor,
                                                         op0=ALU.is_lt, op1=ALU.subtract)
                elif op == 8:
                    ins = nc.vector.scalar_tensor_tensor(out=pyx[:, 0, :], in0=floor[:, 0, :], scalar=-float(WIDE),
                                                         in1=floor[:, 1, :], op0=ALU.mult, op1=ALU.subtract)
                else:
                    ins = nc.vector.tensor_scalar(entry_img[:, row, :].rearrange("p t k -> p (t k)"), pyx[:, 0, :],
                                                  float(RIM * WIDE + RIM), None, ALU.add)
                ins.then_inc(prepped, 1)

            def route(g):
                logits = p_logits.rearrange("p (t e) -> p t e", e=EXPERTS)
                best = top[:, :].rearrange("p (t o) -> p t o", o=1).to_broadcast([P, TILES, EXPERTS])
                dve.wait_ge(logits_done, g + 1)
                nc.vector.tensor_reduce(top[:, :], logits, AX.X, ALU.max).then_inc(routed, 1)
                dve.wait_ge(routed, ROUTE * g + 1)
                nc.vector.tensor_tensor(score[:, :, :], logits, best, ALU.is_ge).then_inc(routed, 1)
                dve.wait_ge(routed, ROUTE * g + 2)
                nc.vector.tensor_tensor(score[:, :, :], score[:, :, :], order[:, :, :], ALU.mult).then_inc(routed, 1)
                dve.wait_ge(routed, ROUTE * g + 3)
                nc.vector.tensor_reduce(top[:, :], score[:, :, :], AX.X, ALU.max).then_inc(routed, 1)
                dve.wait_ge(routed, ROUTE * g + 4)
                dve.wait_ge(mask_done, START + g)
                nc.vector.tensor_tensor(mask[:, :, :], score[:, :, :], best, ALU.is_equal).then_inc(routed, 1)

            def mask_pixels(g, j, e, final):
                every, own, masks, _ = expert_buffers(final, j % COLS)
                dve.wait_ge(mask_done, START + g + 1)
                if final:
                    dve.wait_ge(moe_done, START + EXPERTS * (g - 1))
                else:
                    dve.wait_ge(moe_done, START + EXPERTS * g + (2 if e == 3 else 0))
                nc.vector.tensor_tensor(own[e - 1], every[:, :, :],
                                        by_expert_mask(masks)[:, e - 1:e, :].to_broadcast([P, HALVES, PIX]),
                                        ALU.mult).then_inc(xm_ready, 1)

            def finish_output(q, j, final):
                g = COLS * q + j
                products = expert_buffers(final, j)[3]
                dve.wait_ge(moe_done, START + EXPERTS * (g + 1))
                at = x1[:, bass.ds(q % STRIP_RING, 1), :, :, PATCH * j:PATCH * (j + 1)].rearrange(
                    "p o h r c -> p (o h) r c")
                nc.vector.tensor_tensor(at, products[:, :].rearrange("p (h r c) -> p h r c", h=HALVES, c=PATCH),
                                        at, ALU.add).then_inc(out_ready, 1)

            def x_stat(image, n):
                i, rest = divmod(n, HALVES * STRIP_PIX // STAT_PIX)
                h, c = divmod(rest, STRIP_PIX // STAT_PIX)
                dve.wait_ge(x_in[i], 16 * (image + 1))
                rows = STAT_PIX // SIDE
                at = 1 + PATCH * i + rows * c
                nc.vector.bn_stats(stat_x[:, h, STRIP_PIX // STAT_PIX * i + c, :],
                                   xin[:, h, at:at + rows, :].rearrange("p r c -> p (r c)")).then_inc(x_stats, 1)

            def gn_before(chain, stats):
                base = GN_OPS * chain
                for h in range(HALVES):
                    nc.vector.bn_aggr(mv[:, h, :], stats[:, h, :, :].rearrange("p n v -> p (n v)")).then_inc(gn_dve, 1)
                dve.wait_ge(gn_dve, base + 2)
                nc.vector.tensor_tensor(sq, mv[:, :, 0], mv[:, :, 0], ALU.mult).then_inc(gn_dve, 1)
                dve.wait_ge(gn_dve, base + 3)
                nc.vector.tensor_tensor(mv[:, :, 1], mv[:, :, 1], sq, ALU.add).then_inc(gn_dve, 1)

            def gn_middle(chain):
                base = GN_OPS * chain + GN_A
                dve.wait_ge(gn_sums, chain + 1)
                nc.vector.tensor_copy(gmv[:, :, :].rearrange("p h v -> p (h v)"), p_table[:, 0, 0:2 * HALVES]).then_inc(gn_dve, 1)
                dve.wait_ge(gn_dve, base + 1)
                nc.vector.tensor_tensor(gsq, gmv[:, :, 0], gmv[:, :, 0], ALU.mult).then_inc(gn_dve, 1)
                dve.wait_ge(gn_dve, base + 2)
                nc.vector.tensor_tensor(gvar, gmv[:, :, 1], gsq, ALU.subtract).then_inc(gn_dve, 1)
                dve.wait_ge(gn_dve, base + 3)
                nc.vector.tensor_scalar(gvar, gvar, EPS, None, ALU.add).then_inc(gn_dve, 1)

            def gn_after(chain, scale, shift, below):
                base = GN_OPS * chain + GN_A + GN_B
                dve.wait_ge(gn_root, chain + 1)
                nc.vector.reciprocal(scale[:, :], root).then_inc(gn_dve, 1)
                dve.wait_ge(gn_dve, base + 1)
                nc.vector.scalar_tensor_tensor(out=shift[:, :], in0=gmv[:, :, 0], scalar=-1.0, in1=scale[:, :],
                                               op0=ALU.mult, op1=ALU.mult).then_inc(gn_dve, 1)
                dve.wait_ge(gn_dve, base + 2)
                if below:
                    nc.vector.tensor_copy(shift_below[:, 0:STRIPS - 1, :],
                                          shift[:, :].rearrange("p (o h) -> p o h", o=1)
                                          .to_broadcast([P, STRIPS - 1, HALVES])).then_inc(gn_dve, 1)
                else:
                    nc.vector.tensor_copy(sq, shift[:, :]).then_inc(gn_dve, 1)

            def final_body(step, s, last):
                for j in range(COLS):
                    q = STRIPS * step.expert + s
                    if not (last and j == COLS - 1):
                        route(COLS * q + j + 1)
                        for e in range(1, EXPERTS):
                            mask_pixels(COLS * q + j + 1, j + 1, e, True)
                    finish_output(q, j, True)

            def first_table_body(i, step, s, last):
                pieces = HALVES * STRIP_PIX // STAT_PIX
                if s > 0:
                    for n in range(pieces * (s - 1), pieces * (STRIPS if last else s)):
                        x_stat(step.refill, n)
                if last:
                    dve.wait_ge(x_stats, HALVES * STAT_PIECES * (step.refill + 1))
                    gn_before(chain_of[i, "x"], stat_x)
                dve.wait_ge(prepped, START + PREP * s)
                for op in range(PREP):
                    prepare(s, s, op, offs_banks[s % 2])
                if last:
                    gn_middle(chain_of[i, "x"])
                    gn_after(chain_of[i, "x"], scale_x, shift_x, True)

            def strip_body(i, step, s, first, last):
                if step.only_expert:
                    final_body(step, s, last)
                    return
                if step.only_table:
                    first_table_body(i, step, s, last)
                    return
                for j in range(COLS):
                    for k in range(TAPS):
                        l = TAPS * j + k
                        if step.sample is not None and l == 0 and not first:
                            finish_patch(STRIPS * step.sample + s - 1, s - 1, COLS - 1)
                        if step.sample is not None and not (last and step.last_sample and l + 2 >= PAIRS):
                            blend(STRIPS * step.sample + s, l + 2)
                        if step.table is not None and j == COLS - 1:
                            ops = 4 if last else 2
                            for op in range(ops * k, min(ops * (k + 1), PREP)):
                                prepare(STRIPS * step.table + s, s, op)
                        if step.expert is not None:
                            q = STRIPS * step.expert + s
                            if k == 0:
                                route(COLS * q + j)
                            if k == 2 or k == 4 or k == 6:
                                mask_pixels(COLS * q + j, j, k // 2, False)
                            if k == 0 and j:
                                finish_output(q, j - 1, False)
                            elif k == 0 and not first:
                                finish_output(q - 1, COLS - 1, False)
                        if last and step.refill is not None:
                            if STAT_FROM <= l < STAT_TO:
                                pieces, slots = HALVES * STAT_PIECES, STAT_TO - STAT_FROM
                                for n in range((l - STAT_FROM) * pieces // slots, (l - STAT_FROM + 1) * pieces // slots):
                                    x_stat(step.refill, n)
                            if l == TAPS * (COLS - 1) + 3:
                                dve.wait_ge(x_stats, HALVES * STAT_PIECES * (step.refill + 1))
                                gn_before(chain_of[i, "x"], stat_x)
                            if l == TAPS * (COLS - 1) + 5:
                                gn_middle(chain_of[i, "x"])
                            if l == TAPS * (COLS - 1) + 7:
                                gn_after(chain_of[i, "x"], scale_x, shift_x, True)
                        if step.sample is not None and k == 3 and j:
                            finish_patch(STRIPS * step.sample + s, s, j - 1)

            for i, step in enumerate(STEPS):
                if step.sample == 0:
                    blend(0, 0)
                    blend(0, 1)
                if step.only_expert:
                    route(COLS * STRIPS * step.expert)
                    for e in range(1, EXPERTS):
                        mask_pixels(COLS * STRIPS * step.expert, 0, e, True)
                each_strip(dve, step, lambda s, first, last: strip_body(i, step, s, first, last))
                if step.expert is not None and not step.only_expert:
                    finish_output(STRIPS * step.expert + STRIPS - 1, COLS - 1, False)
                if step.only_refill:
                    dve.wait_ge(consts_in, 16 * CONSTS)
                    nc.vector.tensor_copy(idn_bf[:, :], idn[:, :]).then_inc(consts_made, 1)
                    dve.wait_ge(weights_in, 16 * 3)
                    by_expert = wexp[:, :, :].rearrange("p (e h) n -> p e (h n)", e=EXPERTS)
                    nc.vector.tensor_tensor(by_expert[:, 1:EXPERTS, :], by_expert[:, 1:EXPERTS, :],
                                            by_expert[:, 0:1, :].to_broadcast([P, EXPERTS - 1, HALVES * CH]),
                                            ALU.subtract).then_inc(consts_made, 1)
                    dve.wait_ge(consts_made, 2)
                    nc.vector.tensor_tensor(wexp[:, 0:HALVES, :].rearrange("p h n -> p (h n)"),
                                            wexp[:, 0:HALVES, :].rearrange("p h n -> p (h n)"),
                                            xm[:, 0, :, :].rearrange("p h n -> p (h n)"), ALU.add).then_inc(consts_made, 1)
                if step.sample is not None:
                    finish_patch(STRIPS * step.sample + STRIPS - 1, STRIPS - 1, COLS - 1)
                    dve.wait_ge(x1_stats, HALVES * COLS * STRIPS * (step.sample + 1))
                    gn_before(chain_of[i, "x1"], stat_x1)
                    gn_middle(chain_of[i, "x1"])
                    gn_after(chain_of[i, "x1"], scale_x1, shift_x1, False)


def kernel(x, L0_conv_w_off, L0_conv_w_deform, L1_conv_Wr, L1_conv_We, L1_conv_Ws):
    import numpy as np
    import concourse.bacc as bacc
    from concourse.bass_utils import run_bass_kernel_spmd

    p = np.arange(P)
    tile = np.arange(STRIP_TILES)[None, :, None]
    tap = np.arange(TAPS)[None, None, :]
    py = (tile % TILES) * 8 + p[:, None, None] // PATCH + tap // 3 - 1
    px = (tile // TILES) * PATCH + p[:, None, None] % PATCH + tap % 3 - 1
    position = np.stack([np.broadcast_to(a, (P, STRIP_TILES, TAPS)) for a in (py, px)], 1)
    position = position.reshape(P, 2, STRIP_TILES * TAPS).astype(np.float32)
    strip_row = np.broadcast_to(np.arange(STRIPS) * PATCH, (P, STRIPS)).astype(np.float32)
    ident = np.eye(P, dtype=np.float32)
    group_mean = np.kron(np.eye(P // GROUP), np.full((GROUP, GROUP), 1 / GROUP)).astype(np.float32)
    sum_parts = np.tile(np.eye(P // QUADS, OFFS), (QUADS, 1)).astype(np.float32)
    first_wins = np.broadcast_to(EXPERTS - np.arange(EXPERTS), (P, TILES, EXPERTS)).astype(np.float32)

    arrays = {
        "x_in": np.asarray(x).reshape(IMAGES, HALVES, P, SIDE * SIDE),
        "w_offset": np.asarray(L0_conv_w_off).reshape(OFFS, HALVES, P, TAPS).transpose(2, 3, 1, 0)
        .reshape(P, TAPS * HALVES, OFFS),
        "w_deform": np.asarray(L0_conv_w_deform).reshape(CH, HALVES, P, TAPS).transpose(2, 3, 1, 0)
        .reshape(P, TAPS * HALVES, CH),
        "w_router": np.asarray(L1_conv_Wr).reshape(HALVES, P, EXPERTS).transpose(1, 0, 2),
        "w_expert": np.asarray(L1_conv_We).reshape(EXPERTS, HALVES, P, CH).transpose(2, 0, 1, 3)
        .reshape(P, EXPERTS * HALVES, CH),
        "w_shared": np.asarray(L1_conv_Ws).reshape(HALVES, P, CH).transpose(1, 0, 2),
        "ident": ident, "group_mean": group_mean, "position": position,
        "strip_row": strip_row, "first_wins": first_wins, "sum_parts": sum_parts,
    }
    arrays = {name: np.ascontiguousarray(a) for name, a in arrays.items()}
    nc = bacc.Bacc("TRN2", target_bir_lowering=False, num_devices=1, dynamic_dma_scratch_size=4096)
    args = [nc.dram_tensor(f"{name}_dram", a.shape, mybir.dt.from_np(a.dtype), kind="ExternalInput").ap()
            for name, a in arrays.items()]
    out = nc.dram_tensor("out_dram", (IMAGES, HALVES, P, SIDE * SIDE), F32, kind="ExternalOutput").ap()
    build(nc, *args, out)
    r = run_bass_kernel_spmd(nc, [{f"{name}_dram": a for name, a in arrays.items()}], core_ids=[0])
    return r.results[0]["out_dram"].reshape(IMAGES, CH, SIDE, SIDE)
```
